# Optimizing a Trainium2 kernel written in Bass

```python
import numpy as np
import jax
import jax.numpy as jnp

def _softmax(x, axis=-1):
    return jax.nn.softmax(x, axis=axis)

def _gelu(x):
    return jax.nn.gelu(x, approximate=True)

def _silu(x):
    return jax.nn.silu(x)

def _sigmoid(x):
    return jax.nn.sigmoid(x)

def _layernorm(x, axis=-1, eps=1e-05):
    m = jnp.mean(x, axis=axis, keepdims=True)
    v = jnp.var(x, axis=axis, keepdims=True)
    return (x - m) / jnp.sqrt(v + eps)

def _scatter_add(tgt, idx, src, axis=0):
    return tgt.at[idx].add(src)

def _segment_sum(src, seg, n):
    return jax.ops.segment_sum(src, seg, n)
kernel_name = 'mk_gnn_preln_d2_gnn_r8_095f28'

def setup_inputs(seed: int=0):
    np.random.seed(seed)
    _w = jnp.asarray

    def _rec_inputs():
        import jax
        import jax.numpy as jnp
        _gk = jax.random.key(seed)
        x = -0.0002117 + 1 * jax.random.normal(jax.random.fold_in(_gk, 1), (6250, 512), jnp.float32)
        src = jax.random.randint(jax.random.fold_in(_gk, 2), (100000,), 0, 6250, jnp.int32)
        dst = jax.random.randint(jax.random.fold_in(_gk, 3), (100000,), 0, 6250, jnp.int32)
        _o = jnp.argsort(dst, stable=True)
        src = src[_o]
        dst = dst[_o]
        return (x, src, dst)
    x, src, dst = _rec_inputs()

    def _L0_gnn_setup():
        import jax, jax.numpy as jnp
        import numpy as np
        N_NODES = 6250
        N_EDGES = 100000
        D_IN = 512
        D_OUT = 512
        EPS = 1e-05
        key = jax.random.key(seed)
        k1, k2, k3, k4, k5 = jax.random.split(key, 5)
        x = jax.random.normal(k1, (N_NODES, D_IN), dtype=jnp.float32)
        edge_index = jax.random.randint(k2, (2, N_EDGES), 0, N_NODES, dtype=jnp.int64)
        s = 1.0 / np.sqrt(D_IN)
        W_l = jax.random.uniform(k3, (D_OUT, D_IN), jnp.float32, -s, s)
        b_l = jnp.zeros((D_OUT,), jnp.float32)
        W_r = jax.random.uniform(k4, (D_OUT, D_IN), jnp.float32, -s, s)
        gamma = jnp.ones((D_OUT,), jnp.float32)
        beta = jnp.zeros((D_OUT,), jnp.float32)
        return {'x': x, 'edge_index': edge_index, 'W_l': W_l, 'b_l': b_l, 'W_r': W_r, 'gamma': gamma, 'beta': beta}
    _L0_gnn_all = _L0_gnn_setup()
    _L0_gnn_in = {k: v for k, v in _L0_gnn_all.items() if k in ('W_l', 'b_l', 'W_r', 'gamma', 'beta')}
    del _L0_gnn_all

    def _L1_gnn_setup():
        import jax, jax.numpy as jnp
        import numpy as np
        N_NODES = 5000
        N_EDGES = 80000
        DIM_H = 512
        N_HEADS = 8
        D_HEAD = DIM_H // N_HEADS

        def _exphormer_attn(x, edge_index, Wq, Wk, Wv):
            N, D = x.shape
            H, d = (N_HEADS, D_HEAD)
            Q = (x @ Wq).reshape(N, H, d)
            K = (x @ Wk).reshape(N, H, d)
            V = (x @ Wv).reshape(N, H, d)
            src, dst = (edge_index[0], edge_index[1])
            scale = np.float32(1.0 / np.sqrt(d))
            score = jnp.einsum('ehd,ehd->eh', K[src], Q[dst]) * scale
            score = jnp.exp(jnp.clip(score, -5.0, 5.0))[..., None]
            msg = V[src] * score
            wV = jax.ops.segment_sum(msg, dst, num_segments=N)
            Z = jax.ops.segment_sum(score, dst, num_segments=N)
            return (wV / (Z + 1e-06)).reshape(N, D)
        key = jax.random.key(seed)
        ks = jax.random.split(key, 8)
        x = jax.random.normal(ks[0], (N_NODES, DIM_H), dtype=jnp.float32)
        edge_index = jax.random.randint(ks[1], (2, N_EDGES), 0, N_NODES, dtype=jnp.int32)
        virt_h = jax.random.normal(ks[2], (1, DIM_H), dtype=jnp.float32)
        virt_edge_index = jnp.zeros((2, 1), dtype=jnp.int32)
        s = 1.0 / np.sqrt(DIM_H)
        Wq = jax.random.normal(ks[3], (DIM_H, DIM_H), dtype=jnp.float32) * s
        Wk = jax.random.normal(ks[4], (DIM_H, DIM_H), dtype=jnp.float32) * s
        Wv = jax.random.normal(ks[5], (DIM_H, DIM_H), dtype=jnp.float32) * s
        bn_gamma = jnp.ones((DIM_H,), dtype=jnp.float32)
        bn_beta = jnp.zeros((DIM_H,), dtype=jnp.float32)
        return {'x': x, 'edge_index': edge_index, 'virt_h': virt_h, 'virt_edge_index': virt_edge_index, 'Wq': Wq, 'Wk': Wk, 'Wv': Wv, 'bn_gamma': bn_gamma, 'bn_beta': bn_beta}
    _L1_gnn_all = _L1_gnn_setup()
    _L1_gnn_in = {k: v for k, v in _L1_gnn_all.items() if k in ('virt_h', 'virt_edge_index', 'Wq', 'Wk', 'Wv', 'bn_gamma', 'bn_beta')}
    del _L1_gnn_all
    return {'x': x, 'src': src, 'dst': dst, 'L0_gnn_W_l': _L0_gnn_in['W_l'], 'L0_gnn_b_l': _L0_gnn_in['b_l'], 'L0_gnn_W_r': _L0_gnn_in['W_r'], 'L0_gnn_gamma': _L0_gnn_in['gamma'], 'L0_gnn_beta': _L0_gnn_in['beta'], 'L1_gnn_virt_h': _L1_gnn_in['virt_h'], 'L1_gnn_virt_edge_index': _L1_gnn_in['virt_edge_index'], 'L1_gnn_Wq': _L1_gnn_in['Wq'], 'L1_gnn_Wk': _L1_gnn_in['Wk'], 'L1_gnn_Wv': _L1_gnn_in['Wv'], 'L1_gnn_bn_gamma': _L1_gnn_in['bn_gamma'], 'L1_gnn_bn_beta': _L1_gnn_in['bn_beta']}

def reference(x, src, dst, L0_gnn_W_l, L0_gnn_b_l, L0_gnn_W_r, L0_gnn_gamma, L0_gnn_beta, L1_gnn_virt_h, L1_gnn_virt_edge_index, L1_gnn_Wq, L1_gnn_Wk, L1_gnn_Wv, L1_gnn_bn_gamma, L1_gnn_bn_beta):
    import jax
    import jax.numpy as jnp

    def _L0_gnn_ref(x, edge_index, W_l, b_l, W_r, gamma, beta):
        import jax, jax.numpy as jnp
        import numpy as np
        N_NODES = 6250
        N_EDGES = 100000
        D_IN = 512
        D_OUT = 512
        EPS = 1e-05
        N = x.shape[0]
        src = edge_index[0]
        dst = edge_index[1]
        agg = jax.ops.segment_sum(x[src], dst, num_segments=N)
        deg = jax.ops.segment_sum(jnp.ones_like(dst, jnp.float32), dst, num_segments=N)
        mean_nb = agg / jnp.maximum(deg, 1.0)[:, None]
        h = mean_nb @ W_l.T + b_l + x @ W_r.T
        h = jax.nn.relu(h)
        mu = jnp.mean(h, axis=0)
        var = jnp.mean((h - mu) ** 2, axis=0)
        out = (h - mu) * jax.lax.rsqrt(var + EPS) * gamma + beta
        return out

    def _L1_gnn_ref(x, edge_index, virt_h, virt_edge_index, Wq, Wk, Wv, bn_gamma, bn_beta):
        import jax, jax.numpy as jnp
        import numpy as np
        N_NODES = 5000
        N_EDGES = 80000
        DIM_H = 512
        N_HEADS = 8
        D_HEAD = DIM_H // N_HEADS

        def _exphormer_attn(x, edge_index, Wq, Wk, Wv):
            N, D = x.shape
            H, d = (N_HEADS, D_HEAD)
            Q = (x @ Wq).reshape(N, H, d)
            K = (x @ Wk).reshape(N, H, d)
            V = (x @ Wv).reshape(N, H, d)
            src, dst = (edge_index[0], edge_index[1])
            scale = np.float32(1.0 / np.sqrt(d))
            score = jnp.einsum('ehd,ehd->eh', K[src], Q[dst]) * scale
            score = jnp.exp(jnp.clip(score, -5.0, 5.0))[..., None]
            msg = V[src] * score
            wV = jax.ops.segment_sum(msg, dst, num_segments=N)
            Z = jax.ops.segment_sum(score, dst, num_segments=N)
            return (wV / (Z + 1e-06)).reshape(N, D)
        h_attn = _exphormer_attn(x, edge_index, Wq, Wk, Wv)
        h = x + h_attn
        mean = jnp.mean(h, axis=0)
        var = jnp.mean(jnp.square(h - mean), axis=0)
        return (h - mean) * jax.lax.rsqrt(var + 1e-05) * bn_gamma + bn_beta
    edge_index = jnp.stack([src, dst])
    h = jnp.maximum(_layernorm(x, axis=-1), 0.0)
    x = x + _L0_gnn_ref(h, edge_index, L0_gnn_W_l, L0_gnn_b_l, L0_gnn_W_r, L0_gnn_gamma, L0_gnn_beta)
    h = jnp.maximum(_layernorm(x, axis=-1), 0.0)
    x = x + _L1_gnn_ref(h, edge_index, L1_gnn_virt_h, L1_gnn_virt_edge_index, L1_gnn_Wq, L1_gnn_Wk, L1_gnn_Wv, L1_gnn_bn_gamma, L1_gnn_bn_beta)
    return x

_drawn_inputs = setup_inputs


def setup_inputs(seed=0):
    import zlib

    import numpy as np

    out = dict(_drawn_inputs(seed))
    spreads = {'L0_gnn_b_l': (0.0, 0.1),
     'L0_gnn_gamma': (1.0, 0.2),
     'L0_gnn_beta': (0.0, 0.1),
     'L1_gnn_bn_gamma': (1.0, 0.2),
     'L1_gnn_bn_beta': (0.0, 0.1)}
    factors = {}
    for name, (base, spread) in spreads.items():
        noise = np.random.default_rng([zlib.crc32(name.encode()), seed]).standard_normal(out[name].shape)
        drawn = base * np.exp(spread * noise) if base else spread * noise
        out[name] = jnp.asarray(drawn.astype(out[name].dtype))
    for name, factor in factors.items():
        out[name] = (out[name] * factor).astype(out[name].dtype)
    return out
```

```python
from contextlib import ExitStack

import concourse.bass as bass
from concourse import mybir

F32 = mybir.dt.float32
F32R = mybir.dt.float32r
I32 = mybir.dt.int32
ALU = mybir.AluOpType
ACT = mybir.ActivationFunctionType
AX = mybir.AxisListType.X
ds = bass.ds

P = 128
EPS = 1e-5
HEADS = 8


def build(nc, x, src, dst, W_l, b_l, W_r, gamma0, beta0, Wq, Wk, Wv, gamma1, beta1, out):
    N, D = x.shape
    E = src.shape[0]
    DH = D // HEADS
    KC = D // P
    WINDOWS = -(-N // P)
    LAST = N - (WINDOWS - 1) * P
    WIDTH = D + HEADS
    G = 2
    GE = G * P
    GROUPS = -(-E // GE)
    U = 8
    H = U // 2
    ITERS = -(-(GROUPS + WINDOWS - 1) // U)
    STEPS = ITERS * U
    TCH = -(-(STEPS + U) // P)
    TS = TCH * P
    TAIL = (GROUPS + 1) * GE - E
    OUTSIDE = 1 << 14
    PAIRS = WINDOWS // 2
    assert N <= OUTSIDE and WINDOWS == 2 * PAIRS + 1 and TS <= 512 and GROUPS <= 512 and D == 512

    src_pad = nc.dram_tensor("src_pad", (GROUPS + 1, GE), I32).ap()
    dst_pad = nc.dram_tensor("dst_pad", (GROUPS + 1, GE), I32).ap()
    y_d = nc.dram_tensor("y_d", (WINDOWS * P, D), F32).ap()
    z_d = nc.dram_tensor("z_d", (WINDOWS * P, D), F32).ap()
    h1_d = nc.dram_tensor("h1_d", (WINDOWS * P, D), F32).ap()
    x1_d = nc.dram_tensor("x1_d", (WINDOWS * P, D), F32).ap()
    kv_d = nc.dram_tensor("kv_d", (WINDOWS * P, 2 * D), F32).ap()
    q_d = nc.dram_tensor("q_d", (WINDOWS * P, D), F32).ap()

    def sb(ctx, name, shape, dt=F32):
        return ctx.enter_context(nc.sbuf_tensor(name, shape, dt))

    def pb(ctx, name, shape):
        return ctx.enter_context(nc.psum_tensor(name, shape, F32))

    life = ExitStack()

    def sem(name):
        return life.enter_context(nc.semaphore(name))

    def sems(name, n):
        return [sem(f"{name}{k}") for k in range(n)]

    with life:
        sums = sb(life, "sums", [P, WINDOWS * WIDTH])
        src_t = sb(life, "src_t", [P, TS * G], I32)
        dst_t = sb(life, "dst_t", [P, TS * G], I32)
        rel_t = sb(life, "rel_t", [P, TS * G])
        col_t = sb(life, "col_t", [1, TS], I32)
        ident = sb(life, "ident", [P, P])
        ones = sb(life, "ones", [P, P])
        lane = sb(life, "lane", [P, G, P])
        A_bc = sb(life, "A_bc", [P, D])
        C_bc = sb(life, "C_bc", [P, D])
        S1 = sb(life, "S1", [P, D])
        S2 = sb(life, "S2", [P, D])

        alone_count = sem("alone_count")

        def alone(eng):
            eng.sem_inc(alone_count, 1)

        def window(w, width=D):
            return sums[:, ds(w * WIDTH, width)]

        def nc_block():
            def run(program):
                with nc.Block() as block:
                    program(block)
            return run

        def prepare():
            with ExitStack() as ctx:
                fill = sb(ctx, "fill", [1, 2, TAIL], I32)
                first_i = sb(ctx, "first_i", [1, GROUPS], I32)
                first = sb(ctx, "first", [1, GROUPS])
                bound = sb(ctx, "bound", [P, 1])
                part = sb(ctx, "part", [P, 1])
                before = sb(ctx, "before", [P, GROUPS])
                cnt = sb(ctx, "cnt", [P, 1])
                pos = sb(ctx, "pos", [P, 1])
                step = sb(ctx, "step", [P, TS])
                passed = sb(ctx, "passed", [P, TS])
                grp = sb(ctx, "grp", [1, TS])
                grp_c = sb(ctx, "grp_c", [1, TS])
                neg = sb(ctx, "neg", [1, TS])
                win = sb(ctx, "win", [1, TS])
                grp_col = sb(ctx, "grp_col", [P, TCH], I32)
                win_col = sb(ctx, "win_col", [P, TCH])
                eidx = sb(ctx, "eidx", [P, 2, TCH, GE], I32)
                rel = sb(ctx, "rel", [P, TCH, GE])
                inw = sb(ctx, "inw", [P, TCH, GE])
                off = sb(ctx, "off", [P, TCH, GE])
                idf = sb(ctx, "idf", [P, 2, TCH, GE])
                ps_f = pb(ctx, "ps_f", [P, 512])
                ps_b = pb(ctx, "ps_b", [P, 512])
                ps_c = pb(ctx, "ps_c", [P, 512])
                ps_t = [pb(ctx, f"ps_t{k}", [P, 512]) for k in range(2)]

                filled, padded, got_first = sem("filled"), sem("padded"), sem("got_first")
                made, const = sem("made"), sem("const")
                first_f, first_b, counted = sem("first_f"), sem("first_b"), sem("counted")
                summed_b, table_row, cols_ps, cols_sb = sem("summed_b"), sem("table_row"), sem("cols_ps"), sem("cols_sb")
                rows_got, masked, turned, stored = sem("rows_got"), sem("masked"), sem("turned"), sem("stored")
                chain = sem("chain")

                @nc_block()
                def _(block):
                    @block.sync
                    def _(sp):
                        sp.dma_start(first_i[:, :], dst[:].rearrange("(a e) -> a e", a=1)[:, 0:E:GE],
                                     allow_slow_non_contiguous=True).then_inc(got_first, 16)
                        for pad, given in ((src_pad, src), (dst_pad, dst)):
                            flat = pad.rearrange("a b -> (a b)")
                            sp.dma_start(flat[0:E].rearrange("(a b) -> a b", a=16),
                                         given[:].rearrange("(a b) -> a b", a=16)).then_inc(padded, 16)
                        sp.wait_ge(filled, 2)
                        for k, pad in enumerate((src_pad, dst_pad)):
                            flat = pad.rearrange("a b -> (a b)")
                            sp.dma_start(flat[E:E + TAIL].rearrange("(a b) -> a b", a=1),
                                         fill[:, k, :]).then_inc(padded, 16)

                    @block.gpsimd
                    def _(pool):
                        nc.gpsimd.memset(fill[:, 0, :], 0).then_inc(filled, 1)
                        nc.gpsimd.memset(fill[:, 1, :], WINDOWS * P).then_inc(filled, 1)
                        nc.gpsimd.memset(ident[:, :], 0.0).then_inc(made, 1)
                        nc.gpsimd.memset(ones[:, :], 1.0).then_inc(const, 1)
                        exact = dict(allow_small_or_imprecise_dtypes=True)
                        nc.gpsimd.iota(bound[:, :], pattern=[[0, 1]], base=P, channel_multiplier=P, **exact).then_inc(const, 1)
                        nc.gpsimd.iota(part[:, :], pattern=[[0, 1]], base=0, channel_multiplier=1, **exact).then_inc(const, 1)
                        nc.gpsimd.iota(step[:, :], pattern=[[1, TS]], base=0, channel_multiplier=0, **exact).then_inc(const, 1)
                        nc.gpsimd.iota(lane[:, :, :], pattern=[[0, G], [1, P]], base=0, channel_multiplier=0, **exact).then_inc(const, 1)
                        pool.wait_ge(made, 1)
                        nc.gpsimd.affine_select(out=ident[:, :], in_=ident[:, :], compare_op=ALU.not_equal, fill=1.0,
                                                base=0, pattern=[[-1, P]], channel_multiplier=1).then_inc(const, 1)
                        nc.gpsimd.memset(sums[:, :], 0.0).then_inc(made, 1)
                        pool.wait_ge(padded, 64)
                        pool.wait_ge(cols_sb, 1)
                        for c in range(TCH):
                            for k, pad in enumerate((src_pad, dst_pad)):
                                pool.indirect_dma_start(
                                    eidx[:, k, c, :], None, pad[:, :],
                                    bass.IndirectOffsetOnAxis(grp_col[:, c:c + 1], 0)).then_inc(rows_got, 16)
                        pool.wait_ge(made, 2)

                    @block.tensor
                    def _(pe):
                        pe.wait_ge(const, 6)
                        pe.wait_ge(first_f, 1)
                        nc.tensor.matmul(ps_f[:, 0:GROUPS], ones[0:1, :], first[0:1, :], start=True, stop=True).then_inc(first_b, 1)
                        pe.wait_ge(counted, 1)
                        nc.tensor.matmul(ps_b[:, 0:TS], ones[0:WINDOWS - 1, :], passed[0:WINDOWS - 1, :],
                                         start=True, stop=True).then_inc(summed_b, 1)
                        pe.wait_ge(table_row, 1)
                        for k, row in enumerate((grp_c, win)):
                            for c in range(TCH):
                                last = nc.tensor.matmul(ps_c[:, 2 * (k * TCH + c):2 * (k * TCH + c) + 1],
                                                        row[0:1, c * P:(c + 1) * P], ones[0:1, 0:1], start=True, stop=True)
                        last.then_inc(cols_ps, 1)
                        for n, (table, c) in enumerate((t, c) for t in range(3) for c in range(TCH)):
                            if n < TCH:
                                pe.wait_ge(masked, 3 * c + 3)
                            if n >= 2:
                                pe.wait_ge(stored, n - 1)
                            given = (rel[:, c, :], idf[:, 0, c, :], idf[:, 1, c, :])[table]
                            for g in range(G):
                                last = nc.tensor.transpose(ps_t[n % 2][:, g * P:(g + 1) * P],
                                                           given[:, g * P:(g + 1) * P], ident[:, :])
                            last.then_inc(turned, 1)

                    @block.vector
                    def _(dve):
                        done = [0]

                        def then(ins):
                            done[0] += 1
                            ins.then_inc(chain, 1)
                            dve.wait_ge(chain, done[0])

                        dve.wait_ge(const, 6)
                        dve.wait_ge(got_first, 16)
                        nc.vector.tensor_copy(first[:, :], first_i[:, :]).then_inc(first_f, 1)
                        dve.wait_ge(first_b, 1)
                        then(nc.vector.tensor_scalar(before[:, :], ps_f[:, 0:GROUPS], bound[:, 0:1], None, ALU.is_lt))
                        then(nc.vector.tensor_reduce(cnt[:, :], before[:, :], AX, ALU.add))
                        then(nc.vector.tensor_tensor(pos[:, :], cnt[:, :], part[:, :], ALU.add))
                        nc.vector.tensor_scalar(passed[:, :], step[:, :], pos[:, 0:1], None, ALU.is_ge).then_inc(counted, 1)
                        dve.wait_ge(summed_b, 1)
                        then(nc.vector.tensor_tensor(grp[:, :], step[0:1, :], ps_b[0:1, 0:TS], ALU.subtract))
                        then(nc.vector.tensor_scalar(neg[:, :], grp[:, :], 0.0, None, ALU.is_lt))
                        then(nc.vector.tensor_tensor(win[:, :], ps_b[0:1, 0:TS], neg[:, :], ALU.subtract))
                        then(nc.vector.tensor_scalar(col_t[:, :], win[:, :], float(WIDTH), None, ALU.mult))
                        nc.vector.tensor_scalar(grp_c[:, :], grp[:, :], 0.0, float(GROUPS), ALU.max, ALU.min).then_inc(table_row, 1)
                        dve.wait_ge(cols_ps, 1)
                        then(nc.vector.tensor_copy(grp_col[:, :], ps_c[:, 0:2 * TCH:2]))
                        then(nc.vector.tensor_scalar(win_col[:, :], ps_c[:, 2 * TCH:4 * TCH:2], float(P), None, ALU.mult))
                        dve.sem_inc(cols_sb, 1)

                        dve.wait_ge(rows_got, 16 * 2 * TCH)
                        for c in range(TCH):
                            then(nc.vector.tensor_scalar(rel[:, c, :], eidx[:, 1, c, :], win_col[:, c:c + 1], None, ALU.subtract))
                            then(nc.vector.tensor_scalar(inw[:, c, :], rel[:, c, :], 0.0, None, ALU.is_ge))
                            then(nc.vector.scalar_tensor_tensor(off[:, c, :], rel[:, c, :], float(P), inw[:, c, :],
                                                                ALU.is_lt, ALU.mult))
                            then(nc.vector.tensor_scalar(inw[:, c, :], off[:, c, :], -float(OUTSIDE), float(OUTSIDE),
                                                         ALU.mult, ALU.add))
                            for k in range(2):
                                nc.vector.tensor_tensor(idf[:, k, c, :], eidx[:, k, c, :], inw[:, c, :], ALU.add).then_inc(masked, 1)
                            dve.sem_inc(masked, 1)
                        for n, (table, c) in enumerate((t, c) for t in range(3) for c in range(TCH)):
                            dve.wait_ge(turned, n + 1)
                            to = (rel_t, src_t, dst_t)[table][:, c * P * G:(c + 1) * P * G]
                            nc.vector.tensor_copy(to.rearrange("p (s g) -> p g s", g=G),
                                                  ps_t[n % 2][:, 0:GE].rearrange("p (g s) -> p g s", g=G)).then_inc(stored, 1)

        def dense(layer, given):
            M = len(given)
            tag = str(layer)
            with ExitStack() as ctx:
                w_hi = sb(ctx, "w_hi" + tag, [P, M, KC, D], F32R)
                w_lo = sb(ctx, "w_lo" + tag, [P, M, KC, D], F32R)
                x_sb = sb(ctx, "x_sb" + tag, [P, 2, D])
                x1 = sb(ctx, "x1_sb", [P, 2, D]) if layer else x_sb
                h = sb(ctx, "h" + tag, [P, 2, D])
                st = sb(ctx, "st" + tag, [P, 6])
                mv = sb(ctx, "mv" + tag, [P, 2])
                sd = sb(ctx, "sd" + tag, [P, 1])
                rs = sb(ctx, "rs" + tag, [P, 2])
                nb = sb(ctx, "nb" + tag, [P, 2])
                hT_hi = sb(ctx, "hT_hi" + tag, [P, 2, D], F32R)
                hT_lo = sb(ctx, "hT_lo" + tag, [P, 2, D], F32R)
                o_sb = sb(ctx, "o_sb" + tag, [P, 2, 2, D])
                w_st = o_sb[:, :, :, :].rearrange("p a b d -> p (a b) d")
                if layer:
                    q_sb = sb(ctx, "q_sb", [P, 2, D])
                else:
                    b_row = sb(ctx, "b_row", [1, D])
                    b_bc = sb(ctx, "b_bc", [P, D])
                ps_t = [pb(ctx, f"ps_t{tag}{k}", [P, 512]) for k in range(2)]
                ps_o = [[pb(ctx, f"ps_o{tag}{k}{j}", [P, 512]) for j in range(M)] for k in range(2)]

                w_in, w_turned, w_high, w_split, b_in = (sem(n + tag) for n in ("w_in", "w_turned", "w_high", "w_split", "b_in"))
                x_in, t_made, t_sum, normal = sems("x_in" + tag, 2), sem("t_made" + tag), sem("t_sum" + tag), sem("normal" + tag)
                var_ready, dev_ready, shift_ready, h_made = (sem(n + tag) for n in ("var_ready", "dev_ready", "shift_ready", "h_made"))
                turned, high, split, made, by_act, by_dve = (
                    sem(n + tag) for n in ("turned", "high", "split", "made", "by_act", "by_dve"))
                kept, stored = sems("kept" + tag, 2), sems("stored" + tag, 2)

                def later(w):
                    return not isinstance(w, int) or w >= 2

                @nc_block()
                def _(block):
                    @block.sync
                    def _(sp):
                        def load(w, par, n=P):
                            if later(w):
                                sp.wait_ge(t_made if layer else h_made, w - 1)
                            sp.dma_start(x_sb[0:n, par, :], x[ds(w * P, n), :]).then_inc(x_in[par], 16)

                        def keep(w, par):
                            sp.wait_ge(h_made, w + 1)
                            sp.dma_start(x1_d[ds(w * P, P), :], x1[:, par, :]).then_inc(kept[par], 16)
                            sp.dma_start(h1_d[ds(w * P, P), :], h[:, par, :]).then_inc(kept[par], 16)

                        def store(w, par):
                            sp.wait_ge(by_act, w + 1)
                            sp.wait_ge(by_dve, w + 1)
                            rows = ds(w * P, P)
                            if layer:
                                sp.dma_start(q_d[rows, :], q_sb[:, par, :]).then_inc(stored[par], 16)
                                sp.dma_start(kv_d[rows, :], o_sb[:, par, :, :].rearrange("p a d -> p (a d)")).then_inc(stored[par], 16)
                            else:
                                sp.dma_start(y_d[rows, :], o_sb[:, par, 0, :]).then_inc(stored[par], 16)
                                sp.dma_start(z_d[rows, :], o_sb[:, par, 1, :]).then_inc(stored[par], 16)

                        def both(w, par, n=P):
                            load(w + 2, par, n)
                            if layer:
                                keep(w + 1, 1 - par)
                            store(w, par)

                        load(0, 0)
                        load(1, 1)
                        if not layer:
                            sp.dma_start(b_row[:, :], b_l[:].rearrange("(a n) -> a n", a=1)).then_inc(b_in, 16)
                        for k, w in enumerate(given):
                            if k:
                                sp.wait_ge(w_split, k * KC)
                            sp.dma_start(w_st, w[:, :].rearrange("(c p) i -> p c i", p=P)).then_inc(w_in, 16)
                        if layer:
                            keep(0, 0)
                        both(0, 0)
                        both(1, 1)
                        with sp.Fori(1, PAIRS - 1) as i:
                            for par in range(2):
                                both(2 * i + par, par)
                        both(WINDOWS - 3, 0, LAST)
                        if layer:
                            keep(WINDOWS - 1, 0)
                        store(WINDOWS - 2, 1)
                        store(WINDOWS - 1, 0)
                        for par in range(2):
                            if layer:
                                sp.wait_ge(kept[par], 32 * (PAIRS + 1 - par))
                            sp.wait_ge(stored[par], 32 * (PAIRS + 1 - par))

                    if layer:
                        @block.gpsimd
                        def _(pool):
                            def shift(w, i, par):
                                pool.wait_ge(x_in[par], 16 * (i + 1))
                                nc.gpsimd.tensor_tensor(x_sb[:, par, :], x_sb[:, par, :], C_bc[:, :], ALU.add).then_inc(t_sum, 1)

                            with pool.Fori(0, PAIRS) as i:
                                for par in range(2):
                                    shift(2 * i + par, i, par)
                            shift(WINDOWS - 1, PAIRS, 0)

                    @block.vector
                    def _(dve):
                        def part_low(n, source, lo, hi, of, count):
                            dve.wait_ge(of, n + 1)
                            nc.vector.tensor_tensor(lo, source, hi.bitcast(F32), ALU.subtract).then_inc(count, 1)

                        for k in range(M):
                            for c in range(KC):
                                n = k * KC + c
                                part_low(n, w_st[:, c, :] if layer else ps_o[n % 2][0][:, :],
                                         w_lo[:, k, c, :], w_hi[:, k, c, :], w_high, w_split)
                        if not layer:
                            dve.wait_ge(w_turned, M * KC + 1)
                            nc.vector.tensor_copy(b_bc[:, :], ps_o[0][1][:, :]).then_inc(w_split, 1)
                            dve.wait_ge(w_split, M * KC + 1)

                        def statistics(w, i, par):
                            at = w * 6

                            def then(ins, k):
                                ins.then_inc(normal, 1)
                                dve.wait_ge(normal, at + k)

                            if layer:
                                if later(w):
                                    dve.wait_ge(kept[par], 32 * i)
                                then(nc.vector.tensor_tensor(x1[:, par, :], window(w), A_bc[:, :], ALU.mult), 1)
                                dve.wait_ge(t_sum, w + 1)
                                then(nc.vector.tensor_tensor(x1[:, par, :], x1[:, par, :], x_sb[:, par, :], ALU.add), 2)
                                dve.sem_inc(t_made, 1)
                            else:
                                dve.wait_ge(x_in[par], 16 * (i + 1))
                                dve.sem_inc(normal, 2)
                            then(nc.vector.bn_stats(st[:, :], x1[:, par, :]), 3)
                            alone(dve)
                            then(nc.vector.bn_aggr(mv[:, :], st[:, :]), 4)
                            nc.vector.tensor_scalar(sd[:, :], mv[:, 1:2], EPS, None, ALU.add).then_inc(var_ready, 1)
                            dve.wait_ge(dev_ready, w + 1)
                            if later(w):
                                dve.wait_ge(h_made, w - 1)
                            then(nc.vector.reciprocal(rs[:, par:par + 1], sd[:, :]), 5)
                            then(nc.vector.scalar_tensor_tensor(nb[:, par:par + 1], mv[:, 0:1], -1.0, rs[:, par:par + 1],
                                                                ALU.mult, ALU.mult), 6)
                            dve.sem_inc(shift_ready, 1)

                        def split_h(w, par):
                            if later(w):
                                dve.wait_ge(made, M * (w - 1))
                            part_low(w, ps_t[par][:, :], hT_lo[:, par, :], hT_hi[:, par, :], high, split)

                        def read(w, i, par):
                            dve.wait_ge(made, M * w + 2)
                            if later(w):
                                dve.wait_ge(stored[par], 32 * i)
                            if layer:
                                nc.vector.tensor_copy(o_sb[:, par, 0, :], ps_o[par][1][:, :]).then_inc(by_dve, 1)
                            else:
                                nc.vector.tensor_tensor(o_sb[:, par, 1, :], ps_o[par][1][:, :], b_bc[:, :], ALU.add).then_inc(by_dve, 1)

                        statistics(0, 0, 0)
                        statistics(1, 0, 1)
                        split_h(0, 0)
                        for w in range(2):
                            split_h(w + 1, 1 - w)
                            statistics(w + 2, 1, w)
                            read(w, 0, w)
                        with dve.Fori(1, PAIRS - 1) as i:
                            for par in range(2):
                                split_h(2 * i + par + 1, 1 - par)
                                statistics(2 * i + par + 2, i + 1, par)
                                read(2 * i + par, i, par)
                        for w in range(WINDOWS - 3, WINDOWS):
                            if w < WINDOWS - 1:
                                split_h(w + 1, 1 - w % 2)
                            if w < WINDOWS - 2:
                                statistics(w + 2, w // 2 + 1, w % 2)
                            read(w, w // 2, w % 2)

                    @block.scalar
                    def _(act):
                        for k in range(M):
                            for c in range(KC):
                                n = k * KC + c
                                if layer:
                                    act.wait_ge(w_in, 16 * (k + 1))
                                else:
                                    act.wait_ge(w_turned, n + 1)
                                nc.scalar.copy(w_hi[:, k, c, :], w_st[:, c, :] if layer else ps_o[n % 2][0][:, :]).then_inc(w_high, 1)

                        def norm(w, i, par):
                            act.wait_ge(var_ready, w + 1)
                            nc.scalar.activation(sd[:, :], sd[:, :], ACT.Sqrt).then_inc(dev_ready, 1)
                            act.wait_ge(shift_ready, w + 1)
                            if later(w):
                                if layer:
                                    act.wait_ge(kept[par], 32 * i)
                                act.wait_ge(turned, w - 1)
                            nc.scalar.activation(h[:, par, :], x1[:, par, :], ACT.Relu, bias=nb[:, par:par + 1],
                                                 scale=rs[:, par:par + 1]).then_inc(h_made, 1)

                        def high_h(w, par):
                            act.wait_ge(turned, w + 1)
                            if later(w):
                                act.wait_ge(made, M * (w - 1))
                            nc.scalar.copy(hT_hi[:, par, :], ps_t[par][:, :]).then_inc(high, 1)

                        def read(w, i, par):
                            act.wait_ge(made, M * w + M if layer else M * w + 1)
                            if later(w):
                                act.wait_ge(stored[par], 32 * i)
                            if layer:
                                nc.scalar.activation(q_sb[:, par, :], ps_o[par][0][:, :], ACT.Copy, scale=DH ** -0.5)
                                nc.scalar.copy(o_sb[:, par, 1, :], ps_o[par][2][:, :]).then_inc(by_act, 1)
                            else:
                                nc.scalar.copy(o_sb[:, par, 0, :], ps_o[par][0][:, :]).then_inc(by_act, 1)

                        norm(0, 0, 0)
                        norm(1, 0, 1)
                        high_h(0, 0)
                        for w in range(2):
                            high_h(w + 1, 1 - w)
                            norm(w + 2, 1, w)
                            read(w, 0, w)
                        with act.Fori(1, PAIRS - 1) as i:
                            for par in range(2):
                                high_h(2 * i + par + 1, 1 - par)
                                norm(2 * i + par + 2, i + 1, par)
                                read(2 * i + par, i, par)
                        for w in range(WINDOWS - 3, WINDOWS):
                            if w < WINDOWS - 1:
                                high_h(w + 1, 1 - w % 2)
                            if w < WINDOWS - 2:
                                norm(w + 2, w // 2 + 1, w % 2)
                            read(w, w // 2, w % 2)

                    @block.tensor
                    def _(pe):
                        if not layer:
                            for k in range(M):
                                pe.wait_ge(w_in, 16 * (k + 1))
                                for c in range(KC):
                                    n = k * KC + c
                                    if n >= 2:
                                        pe.wait_ge(w_split, n - 1)
                                    for o in range(KC):
                                        last = nc.tensor.transpose(ps_o[n % 2][0][:, o * P:(o + 1) * P],
                                                                   w_st[:, o, c * P:(c + 1) * P], ident[:, :])
                                    last.then_inc(w_turned, 1)
                            pe.wait_ge(b_in, 16)
                            nc.tensor.matmul(ps_o[0][1][:, :], ones[0:1, :], b_row[0:1, :], start=True, stop=True).then_inc(w_turned, 1)

                        def turn(w, par):
                            pe.wait_ge(h_made, w + 1)
                            if later(w):
                                pe.wait_ge(split, w - 1)
                            for c in range(KC):
                                last = nc.tensor.transpose(ps_t[par][:, c * P:(c + 1) * P], h[:, par, c * P:(c + 1) * P], ident[:, :])
                            last.then_inc(turned, 1)

                        def products(w, par):
                            pe.wait_ge(split, w + 1)
                            if later(w):
                                pe.wait_ge(by_dve, w - 1)
                                pe.wait_ge(by_act, w - 1)
                            for k in range(M):
                                for c in range(KC):
                                    hi, lo = (t[:, par, c * P:(c + 1) * P] for t in (hT_hi, hT_lo))
                                    for j, (a, b) in enumerate(((hi, w_hi), (hi, w_lo), (lo, w_hi))):
                                        last = nc.tensor.matmul(ps_o[par][k][:, :], a, b[:, k, c, :],
                                                                start=(c == 0 and j == 0), stop=(c == KC - 1 and j == 2))
                                last.then_inc(made, 1)

                        turn(0, 0)
                        pe.wait_ge(w_split, M * KC + (0 if layer else 1))
                        for w in range(2):
                            turn(w + 1, 1 - w)
                            products(w, w)
                        with pe.Fori(1, PAIRS) as i:
                            for par in range(2):
                                turn(2 * i + par + 1, 1 - par)
                                products(2 * i + par, par)
                        products(WINDOWS - 1, 0)

        def aggregate():
            with ExitStack() as ctx:
                rows = sb(ctx, "rows", [P, U, G, D])
                hot = sb(ctx, "hot", [P, 4, G, P])
                idx = sb(ctx, "idx", [P, 2, H * G], I32)
                pss = [pb(ctx, f"pss{k}", [P, 1024]) for k in range(4)]
                cleared, staged, rows_in = sem("cleared"), sem("staged"), sems("rows_in", U)
                hot_made, ps_made, ps_free = sem("hot_made"), sem("ps_made"), sem("ps_free")

                @nc_block()
                def _(block):
                    @block.scalar
                    def _(act):
                        def stage(i, half):
                            nc.scalar.copy(idx[:, half, :], src_t[:, ds((i * U + half * H) * G, H * G)]).then_inc(staged, 1)

                        for half in range(2):
                            stage(0, half)
                        with act.Fori(0, ITERS) as i:
                            for half in range(2):
                                for u in range(half * H, half * H + H):
                                    act.wait_ge(rows_in[u], (i + 1) * 16 * G)
                                alone(act)
                                stage(i + 1, half)

                    @block.gpsimd
                    def _(pool):
                        limit = pool.alloc_register("limit0")
                        pool.reg_mov(limit, N - 1)
                        pool.wait_ge(cleared, 1)
                        with pool.Fori(0, ITERS) as i:
                            for u in range(U):
                                if u % H == 0:
                                    pool.wait_ge(staged, i * 2 + u // H + 1)
                                pool.wait_ge(ps_made, i * U + u + 1)
                                alone(pool)
                                for g in range(G):
                                    k = (u % H) * G + g
                                    pool.indirect_dma_start(rows[:, u, g, :], None, y_d[0:N, :],
                                                            bass.IndirectOffsetOnAxis(idx[:, u // H, k:k + 1], 0),
                                                            bounds_check=limit, oob_is_err=False).then_inc(rows_in[u], 16)

                    @block.vector
                    def _(dve):
                        nc.vector.memset(rows[:, :, :, :], 0.0).then_inc(cleared, 1)
                        dve.sem_inc(ps_free, 4)

                        def one_hot(i, u):
                            s = i * U + u
                            dve.wait_ge(ps_made, s + U - 3)
                            nc.vector.tensor_tensor(hot[:, u % 4, :, :], lane[:, :, :],
                                                    rel_t[:, ds(s * G, G)].unsqueeze(2).to_broadcast([P, G, P]),
                                                    ALU.is_equal).then_inc(hot_made, 1)

                        def add(s, u, col):
                            dve.wait_ge(ps_made, s + U + 1)
                            dve.wait_ge(ps_free, s + 4)
                            to = sums[:, ds(col, D + 1)]
                            nc.vector.tensor_tensor(to, to, pss[u % 4][:, 0:D + 1], ALU.add).then_inc(ps_free, 1)

                        cols = load_cols(dve, 0, U)
                        for u in range(U):
                            one_hot(0, u)
                            if u >= 2:
                                add(u - 2, u - 2, cols[u - 2])
                        with dve.Fori(1, ITERS) as i:
                            cols = load_cols(dve, i * U - 2, U)
                            for u in range(U):
                                one_hot(i, u)
                                add(i * U + u - 2, u + 2, cols[u])
                        cols = load_cols(dve, STEPS - 2, 2)
                        for k in range(2):
                            add(STEPS - 2 + k, U - 2 + k, cols[k])

                    @block.tensor
                    def _(pe):
                        pe.sem_inc(ps_made, U)
                        with pe.Fori(0, ITERS) as i:
                            for u in range(U):
                                s = i * U + u
                                ps = pss[u % 4]
                                pe.wait_ge(hot_made, s + 1)
                                pe.wait_ge(ps_free, s + 1)
                                for g in range(G):
                                    last = nc.tensor.matmul(ps[:, D:D + 2], hot[:, u % 4, g, :], ones[:, 0:2],
                                                            start=(g == 0), stop=(g == G - 1))
                                pe.wait_ge(rows_in[u], (i + 1) * 16 * G)
                                for g in range(G):
                                    last = nc.tensor.matmul(ps[:, 0:D], hot[:, u % 4, g, :], rows[:, u, g, :],
                                                            start=(g == 0), stop=(g == G - 1))
                                last.then_inc(ps_made, 1)

        def load_cols(dve, s, n):
            _, cols = nc.values_load_multi_w_load_instructions(
                col_t[0:1, ds(s, n)], engines=[mybir.EngineType.DVE], min_val=0, max_val=(WINDOWS - 1) * WIDTH,
                skip_runtime_bounds_check_because="a step's window is one of 0..WINDOWS-1 by how the table is made")
            return cols

        def combine():
            with ExitStack() as ctx:
                z = sb(ctx, "z_sb", [P, 2, D])
                rd = sb(ctx, "rd", [P, WINDOWS])
                sq = sb(ctx, "sq", [P, 2, D])
                z_in, degrees, added_z, rect, squared, zero1, zero2, summed1, summed2 = (
                    sems("z_in", 2), sem("degrees"), sem("added_z"), sem("rect"), sem("squared"), sem("zero1"), sem("zero2"),
                    sem("summed1"), sem("summed2"))

                @nc_block()
                def _(block):
                    @block.sync
                    def _(sp):
                        def load(w, par):
                            sp.wait_ge(added_z, w + 1)
                            sp.dma_start(z[:, par, :], z_d[ds(w * P, P), :]).then_inc(z_in[par], 16)

                        with sp.Fori(0, PAIRS) as i:
                            for par in range(2):
                                load(2 * i + par, par)
                        load(WINDOWS - 1, 0)

                    @block.vector
                    def _(dve):
                        nc.vector.memset(S1[:, :], 0.0).then_inc(zero1, 1)
                        degree = sums[:, :].rearrange("p (w c) -> p w c", c=WIDTH)[:, :, D]
                        nc.vector.tensor_scalar(rd[:, :], degree, 1.0, None, ALU.max).then_inc(degrees, 1)
                        dve.wait_ge(degrees, 1)
                        nc.vector.reciprocal(rd[:, :], rd[:, :]).then_inc(degrees, 1)
                        dve.wait_ge(degrees, 2)
                        dve.wait_ge(zero1, 1)
                        spread = sums[:, :].rearrange("p (w c) -> p w c", c=WIDTH)[:, :, D + 1]
                        nc.vector.tensor_copy(spread, rd[:, :]).then_inc(degrees, 1)
                        dve.wait_ge(degrees, 3)
                        dve.sem_inc(added_z, 2)

                        def add_z(w, i, par):
                            dve.wait_ge(z_in[par], 16 * (i + 1))
                            alone(dve)
                            nc.vector.scalar_tensor_tensor(window(w), window(w), sums[:, ds(w * WIDTH + D + 1, 1)], z[:, par, :],
                                                           ALU.mult, ALU.add).then_inc(added_z, 1)

                        def add_h(w, n=P):
                            dve.wait_ge(rect, w + 1)
                            nc.vector.tensor_tensor(S1[0:n, :], S1[0:n, :], window(w)[0:n, :], ALU.add).then_inc(summed1, 1)
                            dve.wait_ge(summed1, w + 1)

                        add_z(0, 0, 0)
                        with dve.Fori(0, PAIRS) as i:
                            for par in range(2):
                                add_z(2 * i + par + 1, i + par, 1 - par)
                                add_h(2 * i + par)
                        add_h(WINDOWS - 1, LAST)

                    @block.scalar
                    def _(act):
                        def rectify(w, i, par):
                            act.wait_ge(added_z, w + 3)
                            alone(act)
                            nc.scalar.activation(window(w), window(w), ACT.Relu).then_inc(rect, 1)
                            act.wait_ge(rect, w + 1)
                            if not isinstance(i, int) or i:
                                act.wait_ge(summed2, w - 1)
                            alone(act)
                            nc.scalar.activation(sq[:, par, :], window(w), ACT.Square).then_inc(squared, 1)

                        rectify(0, 0, 0)
                        rectify(1, 0, 1)
                        with act.Fori(1, PAIRS) as i:
                            for par in range(2):
                                rectify(2 * i + par, i, par)
                        rectify(WINDOWS - 1, PAIRS, 0)

                    @block.gpsimd
                    def _(pool):
                        nc.gpsimd.memset(S2[:, :], 0.0).then_inc(zero2, 1)
                        pool.wait_ge(zero2, 1)

                        def add_square(w, par, n=P):
                            pool.wait_ge(squared, w + 1)
                            nc.gpsimd.tensor_tensor(S2[0:n, :], S2[0:n, :], sq[0:n, par, :], ALU.add).then_inc(summed2, 1)
                            pool.wait_ge(summed2, w + 1)

                        with pool.Fori(0, PAIRS) as i:
                            for par in range(2):
                                add_square(2 * i + par, par)
                        add_square(WINDOWS - 1, 0, LAST)

        def coefficients(tag, gamma, beta):
            with ExitStack() as ctx:
                gb = sb(ctx, "gb" + tag, [1, 2, D])
                mu = sb(ctx, "mu" + tag, [P, D])
                var = sb(ctx, "var" + tag, [P, D])
                ps_s = [pb(ctx, f"ps_s{tag}{k}", [P, 512]) for k in range(4)]
                gb_in, tot, chain, var_ready, dev_ready = (sem(n + tag) for n in ("gb_in", "tot", "cchain", "bn_var", "bn_dev"))

                @nc_block()
                def _(block):
                    @block.sync
                    def _(sp):
                        for k, v in enumerate((gamma, beta)):
                            sp.dma_start(gb[:, k, :], v[:].rearrange("(a n) -> a n", a=1)).then_inc(gb_in, 16)

                    @block.tensor
                    def _(pe):
                        nc.tensor.matmul(ps_s[0][:, :], ones[:, :], S1[:, :], start=True, stop=True).then_inc(tot, 1)
                        nc.tensor.matmul(ps_s[1][:, :], ones[:, :], S2[:, :], start=True, stop=True).then_inc(tot, 1)
                        pe.wait_ge(gb_in, 32)
                        for k in range(2):
                            nc.tensor.matmul(ps_s[2 + k][:, :], ones[0:1, :], gb[0:1, k, :], start=True, stop=True).then_inc(tot, 1)

                    @block.vector
                    def _(dve):
                        done = [0]

                        def then(ins):
                            done[0] += 1
                            ins.then_inc(chain, 1)
                            dve.wait_ge(chain, done[0])

                        dve.wait_ge(tot, 1)
                        then(nc.vector.tensor_scalar(mu[:, :], ps_s[0][:, :], 1.0 / N, None, ALU.mult))
                        then(nc.vector.tensor_tensor(var[:, :], mu[:, :], mu[:, :], ALU.mult))
                        dve.wait_ge(tot, 2)
                        then(nc.vector.scalar_tensor_tensor(var[:, :], ps_s[1][:, :], 1.0 / N, var[:, :], ALU.mult, ALU.subtract))
                        nc.vector.tensor_scalar(var[:, :], var[:, :], 0.0, EPS, ALU.max, ALU.add).then_inc(var_ready, 1)
                        dve.wait_ge(dev_ready, 1)
                        then(nc.vector.reciprocal(var[:, :], var[:, :]))
                        dve.wait_ge(tot, 4)
                        then(nc.vector.tensor_tensor(A_bc[:, :], ps_s[2][:, :], var[:, :], ALU.mult))
                        then(nc.vector.tensor_tensor(mu[:, :], mu[:, :], A_bc[:, :], ALU.mult))
                        then(nc.vector.tensor_tensor(C_bc[:, :], ps_s[3][:, :], mu[:, :], ALU.subtract))

                    @block.scalar
                    def _(act):
                        act.wait_ge(var_ready, 1)
                        nc.scalar.activation(var[:, :], var[:, :], ACT.Sqrt).then_inc(dev_ready, 1)

        def attend():
            with ExitStack() as ctx:
                R = 4
                kv = sb(ctx, "kv", [P, R, G, 2 * D])
                q = sb(ctx, "q", [P, R, G, D])
                hot = sb(ctx, "hot1", [P, R, G, P])
                score = sb(ctx, "score", [P, R, G * HEADS])
                wgt = sb(ctx, "wgt", [P, R, G * HEADS])
                idx = sb(ctx, "idx1", [P, 2, 2, H * G], I32)
                pss = [pb(ctx, f"psa{k}", [P, 1024]) for k in range(4)]
                cleared, zeroed, staged, rows_in = sem("cleared1"), sem("zeroed1"), sem("staged1"), sems("kvq_in", R)
                hot_made, ps_made, ps_free = sem("hot_made1"), sem("ps_made1"), sem("ps_free1")
                prod, red, clipped, weighed, scaled = sem("prod"), sem("red"), sem("clipped"), sem("weighed"), sem("scaled")

                @nc_block()
                def _(block):
                    @block.scalar
                    def _(act):
                        def stage(i, half):
                            at = ds((i * U + half * H) * G, H * G)
                            nc.scalar.copy(idx[:, half, 0, :], src_t[:, at])
                            nc.scalar.copy(idx[:, half, 1, :], dst_t[:, at]).then_inc(staged, 1)

                        def weigh(i, u):
                            s = i * U + u
                            act.wait_ge(clipped, s + 1)
                            act.wait_ge(ps_made, s + 1)
                            nc.scalar.activation(wgt[:, u % R, :], score[:, u % R, :], ACT.Exp).then_inc(weighed, 1)

                        for half in range(2):
                            stage(0, half)
                        with act.Fori(0, ITERS) as i:
                            for u in range(U):
                                weigh(i, u)
                                if u % H == H - 1:
                                    for r in range(R):
                                        act.wait_ge(rows_in[r], (i * 2 + u // H + 1) * 32 * G)
                                    alone(act)
                                    stage(i + 1, u // H)

                    @block.gpsimd
                    def _(pool):
                        limit = pool.alloc_register("limit1")
                        pool.reg_mov(limit, N - 1)
                        pool.wait_ge(cleared, 2)
                        with pool.Fori(0, ITERS) as i:
                            for u in range(U):
                                if u % H == 0:
                                    pool.wait_ge(staged, i * 2 + u // H + 1)
                                pool.wait_ge(ps_made, i * U + u + 1)
                                alone(pool)
                                for g in range(G):
                                    k = (u % H) * G + g
                                    for to, table, which in ((kv, kv_d, 0), (q, q_d, 1)):
                                        pool.indirect_dma_start(to[:, u % R, g, :], None, table[0:N, :],
                                                                bass.IndirectOffsetOnAxis(idx[:, u // H, which, k:k + 1], 0),
                                                                bounds_check=limit, oob_is_err=False).then_inc(rows_in[u % R], 16)

                    @block.vector
                    def _(dve):
                        nc.vector.memset(kv[:, :, :, :], 0.0).then_inc(cleared, 1)
                        nc.vector.memset(q[:, :, :, :], 0.0).then_inc(cleared, 1)
                        nc.vector.memset(sums[:, :], 0.0).then_inc(zeroed, 1)
                        dve.wait_ge(zeroed, 1)
                        dve.sem_inc(ps_free, 4)

                        def begin(i, u):
                            s = i * U + u
                            r = u % R
                            dve.wait_ge(ps_made, s + 1)
                            nc.vector.tensor_tensor(hot[:, r, :, :], lane[:, :, :],
                                                    rel_t[:, ds(s * G, G)].unsqueeze(2).to_broadcast([P, G, P]),
                                                    ALU.is_equal).then_inc(hot_made, 1)
                            dve.wait_ge(rows_in[r], (i * 2 + u // R + 1) * 32 * G)
                            nc.vector.tensor_tensor(q[:, r, :, :], q[:, r, :, :], kv[:, r, :, 0:D], ALU.mult).then_inc(prod, 1)

                        def reduce(i, u):
                            s = i * U + u
                            r = u % R
                            dve.wait_ge(prod, s + 1)
                            if not isinstance(i, int) or u >= R:
                                dve.wait_ge(weighed, s - R + 1)
                            nc.vector.tensor_reduce(score[:, r, :], q[:, r, :, :].rearrange("p g (h d) -> p (g h) d", h=HEADS),
                                                    AX, ALU.add).then_inc(red, 1)

                        def clip(i, u):
                            s = i * U + u
                            dve.wait_ge(red, s + 1)
                            nc.vector.tensor_scalar(score[:, u % R, :], score[:, u % R, :], -5.0, 5.0, ALU.max, ALU.min).then_inc(clipped, 1)

                        def scale(s, u):
                            r = u % R
                            dve.wait_ge(weighed, s + 1)
                            w = wgt[:, r, :].rearrange("p (g h) -> p g h", g=G)
                            for g in range(G):
                                v = kv[:, r, g, D:2 * D].rearrange("p (h d) -> p h d", h=HEADS)
                                last = nc.vector.tensor_tensor(v, v, w[:, g, :].unsqueeze(2).to_broadcast([P, HEADS, DH]), ALU.mult)
                            last.then_inc(scaled, 1)

                        def add(s, u, col):
                            dve.wait_ge(ps_made, s + R + 1)
                            dve.wait_ge(ps_free, s + 4)
                            to = sums[:, ds(col, WIDTH)]
                            nc.vector.tensor_tensor(to, to, pss[u % 4][:, 0:WIDTH], ALU.add).then_inc(ps_free, 1)

                        cols = load_cols(dve, 0, U)
                        for u in range(U):
                            begin(0, u)
                            if u >= 1:
                                scale(u - 1, u - 1)
                            reduce(0, u)
                            if u >= 2:
                                add(u - 2, u - 2, cols[u - 2])
                            clip(0, u)
                        with dve.Fori(1, ITERS) as i:
                            cols = load_cols(dve, i * U - 2, U)
                            for u in range(U):
                                begin(i, u)
                                scale(i * U + u - 1, u + U - 1)
                                reduce(i, u)
                                add(i * U + u - 2, u + U - 2, cols[u])
                                clip(i, u)
                        cols = load_cols(dve, STEPS - 2, 2)
                        scale(STEPS - 1, U - 1)
                        for k in range(2):
                            add(STEPS - 2 + k, U - 2 + k, cols[k])

                    @block.tensor
                    def _(pe):
                        pe.sem_inc(ps_made, R)
                        with pe.Fori(0, ITERS) as i:
                            for u in range(U):
                                s = i * U + u
                                r = u % R
                                ps = pss[u % 4]
                                pe.wait_ge(hot_made, s + 1)
                                pe.wait_ge(ps_free, s + 1)
                                pe.wait_ge(weighed, s + 1)
                                for g in range(G):
                                    nc.tensor.matmul(ps[:, D:WIDTH], hot[:, r, g, :], wgt[:, r, g * HEADS:(g + 1) * HEADS],
                                                     start=(g == 0), stop=(g == G - 1))
                                pe.wait_ge(scaled, s + 1)
                                for g in range(G):
                                    last = nc.tensor.matmul(ps[:, 0:D], hot[:, r, g, :], kv[:, r, g, D:2 * D],
                                                            start=(g == 0), stop=(g == G - 1))
                                last.then_inc(ps_made, 1)

        def attended():
            with ExitStack() as ctx:
                h1 = sb(ctx, "h1b", [P, 2, D])
                zr = sb(ctx, "zr", [P, 2, HEADS])
                sq = sb(ctx, "sq1", [P, 2, D])
                zeroed1, zeroed2, h_in, chain, made, squared, added = (
                    sem("zeroed_S1"), sem("zeroed_S2"), sems("h_in2", 2), sem("achain"), sem("h_made"), sem("squared1"), sem("added1"))

                @nc_block()
                def _(block):
                    @block.sync
                    def _(sp):
                        def load(w, par, n=P):
                            sp.wait_ge(made, w + 1)
                            sp.dma_start(h1[0:n, par, :], h1_d[ds(w * P, n), :]).then_inc(h_in[par], 16)

                        with sp.Fori(0, PAIRS) as i:
                            for par in range(2):
                                load(2 * i + par, par)
                        load(WINDOWS - 1, 0)

                    @block.gpsimd
                    def _(pool):
                        nc.gpsimd.memset(S2[:, :], 0.0).then_inc(zeroed2, 1)
                        pool.wait_ge(zeroed2, 1)

                        def add(w, par, n=P):
                            pool.wait_ge(squared, w + 1)
                            nc.gpsimd.tensor_tensor(S2[0:n, :], S2[0:n, :], sq[0:n, par, :], ALU.add).then_inc(added, 1)
                            pool.wait_ge(added, w + 1)

                        with pool.Fori(0, PAIRS) as i:
                            for par in range(2):
                                add(2 * i + par, par)
                        add(WINDOWS - 1, 0, LAST)

                    @block.scalar
                    def _(act):
                        def square(w, par):
                            act.wait_ge(made, w + 3)
                            if not isinstance(w, int) or w >= 2:
                                act.wait_ge(added, w - 1)
                            alone(act)
                            nc.scalar.activation(sq[:, par, :], window(w), ACT.Square).then_inc(squared, 1)

                        square(0, 0)
                        square(1, 1)
                        with act.Fori(1, PAIRS) as i:
                            for par in range(2):
                                square(2 * i + par, par)
                        square(WINDOWS - 1, 0)

                    @block.vector
                    def _(dve):
                        dve.sem_inc(made, 2)
                        nc.vector.memset(S1[:, :], 0.0).then_inc(zeroed1, 1)
                        dve.wait_ge(zeroed1, 1)
                        K = 5

                        def combine(w, i, par, n=P):
                            def then(ins, k):
                                ins.then_inc(chain, 1)
                                dve.wait_ge(chain, w * K + k)

                            then(nc.vector.tensor_scalar(zr[:, par, :], sums[:, ds(w * WIDTH + D, HEADS)], 1e-6, None, ALU.add), 1)
                            then(nc.vector.reciprocal(zr[:, par, :], zr[:, par, :]), 2)
                            v = window(w).rearrange("p (h d) -> p h d", h=HEADS)
                            then(nc.vector.tensor_tensor(v, v, zr[:, par, :].unsqueeze(2).to_broadcast([P, HEADS, DH]), ALU.mult), 3)
                            dve.wait_ge(h_in[par], 16 * (i + 1))
                            then(nc.vector.tensor_tensor(window(w), window(w), h1[:, par, :], ALU.add), 4)
                            dve.sem_inc(made, 1)
                            then(nc.vector.tensor_tensor(S1[0:n, :], S1[0:n, :], window(w)[0:n, :], ALU.add), 5)

                        with dve.Fori(0, PAIRS) as i:
                            for par in range(2):
                                combine(2 * i + par, i, par)
                        combine(WINDOWS - 1, PAIRS, 0, LAST)

        def finish():
            with ExitStack() as ctx:
                x1 = sb(ctx, "x1b", [P, 2, D])
                o = sb(ctx, "o", [P, 2, D])
                x_in, shifted, scaled, done, stored = sems("x_in3", 2), sem("shifted"), sem("scaled1"), sem("done"), sems("stored_", 2)

                @nc_block()
                def _(block):
                    @block.sync
                    def _(sp):
                        def load(w, par):
                            sp.wait_ge(done, w + 1)
                            sp.dma_start(x1[:, par, :], x1_d[ds(w * P, P), :]).then_inc(x_in[par], 16)

                        with sp.Fori(0, PAIRS) as i:
                            for par in range(2):
                                load(2 * i + par, par)
                        load(WINDOWS - 1, 0)

                    @block.scalar
                    def _(act):
                        def store(w, par, n=P):
                            act.wait_ge(done, w + 3)
                            act.dma_start(out[ds(w * P, n), :], o[0:n, par, :]).then_inc(stored[par], 16)

                        with act.Fori(0, PAIRS) as i:
                            for par in range(2):
                                store(2 * i + par, par)
                        store(WINDOWS - 1, 0, LAST)
                        for par in range(2):
                            act.wait_ge(stored[par], 16 * (PAIRS + 1 - par))

                    @block.gpsimd
                    def _(pool):
                        def shift(w, i, par):
                            pool.wait_ge(x_in[par], 16 * (i + 1))
                            nc.gpsimd.tensor_tensor(x1[:, par, :], x1[:, par, :], C_bc[:, :], ALU.add).then_inc(shifted, 1)

                        with pool.Fori(0, PAIRS) as i:
                            for par in range(2):
                                shift(2 * i + par, i, par)
                        shift(WINDOWS - 1, PAIRS, 0)

                    @block.vector
                    def _(dve):
                        dve.sem_inc(done, 2)

                        def scale(w):
                            nc.vector.tensor_tensor(window(w), window(w), A_bc[:, :], ALU.mult).then_inc(scaled, 1)

                        def add(w, i, par):
                            dve.wait_ge(shifted, w + 1)
                            dve.wait_ge(scaled, w + 1)
                            if not isinstance(i, int) or i:
                                dve.wait_ge(stored[par], 16 * i)
                            nc.vector.tensor_tensor(o[:, par, :], window(w), x1[:, par, :], ALU.add).then_inc(done, 1)

                        scale(0)
                        for w in range(2):
                            scale(w + 1)
                            add(w, 0, w)
                        with dve.Fori(1, PAIRS) as i:
                            for par in range(2):
                                scale(2 * i + par + 1)
                                add(2 * i + par, i, par)
                        add(WINDOWS - 1, PAIRS, 0)

        prepare()
        dense(0, (W_l, W_r))
        aggregate()
        combine()
        coefficients("0", gamma0, beta0)
        dense(1, (Wq, Wk, Wv))
        attend()
        attended()
        coefficients("1", gamma1, beta1)
        finish()


def kernel(**inputs):
    import numpy as np
    import concourse.bacc as bacc
    from concourse.bass_utils import run_bass_kernel_spmd

    names = ["x", "src", "dst", "L0_gnn_W_l", "L0_gnn_b_l", "L0_gnn_W_r", "L0_gnn_gamma", "L0_gnn_beta",
             "L1_gnn_Wq", "L1_gnn_Wk", "L1_gnn_Wv", "L1_gnn_bn_gamma", "L1_gnn_bn_beta"]
    nc = bacc.Bacc("TRN2", target_bir_lowering=False, num_devices=1)
    arrays, args = {}, []
    for name in names:
        a = np.ascontiguousarray(inputs[name])
        arrays["in_" + name] = a
        args.append(nc.dram_tensor("in_" + name, a.shape, mybir.dt.from_np(a.dtype), kind="ExternalInput").ap())
    shape = inputs["x"].shape
    result = nc.dram_tensor("result", shape, F32, kind="ExternalOutput").ap()
    build(nc, *args, result)
    r = run_bass_kernel_spmd(nc, [arrays], core_ids=[0])
    return r.results[0]["result"]
```

```python
from contextlib import ExitStack

import concourse.bass as bass
from concourse import mybir

F32 = mybir.dt.float32
F32R = mybir.dt.float32r
I32 = mybir.dt.int32
I16 = mybir.dt.int16
ALU = mybir.AluOpType
ACT = mybir.ActivationFunctionType
AX = mybir.AxisListType.X
ds = bass.ds

P = 128
EPS = 1e-5
HEADS = 8


def build(nc, x, src, dst, W_l, b_l, W_r, gamma0, beta0, Wq, Wk, Wv, gamma1, beta1, out):
    N, D = x.shape
    E = src.shape[0]
    DH = D // HEADS
    KC = D // P
    WINDOWS = -(-N // P)
    LAST = N - (WINDOWS - 1) * P
    WIDTH = D + HEADS
    G = 2
    GE = G * P
    GROUPS = -(-E // GE)
    U = 8
    H = U // 2
    ITERS = -(-(GROUPS + WINDOWS - 1) // U)
    STEPS = ITERS * U
    TCH = -(-(STEPS + U) // P)
    TS = TCH * P
    TAIL = (GROUPS + 1) * GE - E
    OUTSIDE = 1 << 14
    PAIRS = WINDOWS // 2
    QB = 4
    assert WINDOWS * WIDTH < 1 << 15 and N <= OUTSIDE and WINDOWS == 2 * PAIRS + 1 and TS <= 512 and GROUPS <= 512 and D == 512

    src_pad = nc.dram_tensor("src_pad", (GROUPS + 1, GE), I32).ap()
    dst_pad = nc.dram_tensor("dst_pad", (GROUPS + 1, GE), I32).ap()
    y_d = nc.dram_tensor("y_d", (WINDOWS * P, D), F32).ap()
    z_d = nc.dram_tensor("z_d", (WINDOWS * P, D), F32).ap()
    h1_d = nc.dram_tensor("h1_d", (WINDOWS * P, D), F32).ap()
    x1_d = nc.dram_tensor("x1_d", (WINDOWS * P, D), F32).ap()
    kv_d = nc.dram_tensor("kv_d", (WINDOWS * P, 2 * D), F32).ap()
    q_d = nc.dram_tensor("q_d", (WINDOWS * P, 2 * D), F32).ap()

    def sb(ctx, name, shape, dt=F32):
        return ctx.enter_context(nc.sbuf_tensor(name, shape, dt))

    def pb(ctx, name, shape):
        return ctx.enter_context(nc.psum_tensor(name, shape, F32))

    life = ExitStack()

    def sem(name):
        return life.enter_context(nc.semaphore(name))

    def sems(name, n):
        return [sem(f"{name}{k}") for k in range(n)]

    with life:
        sums = sb(life, "sums", [P, WINDOWS * WIDTH])
        src_t = sb(life, "src_t", [P, TS * G], I32)
        rel_t = sb(life, "rel_t", [P, TS * G])
        col_t = sb(life, "col_t", [1, TS], I16)
        row_t = sb(life, "row_t", [1, TS], I16)
        qcol_t = sb(life, "qcol_t", [1, TS], I16)
        new_t = sb(life, "new_t", [1, TS], I16)
        ident = sb(life, "ident", [P, P])
        ones = sb(life, "ones", [P, P])
        lane = sb(life, "lane", [P, P])

        alone_count = sem("alone_count")

        def alone(eng):
            eng.sem_inc(alone_count, 1)

        def window(w, width=D):
            return sums[:, ds(w * WIDTH, width)]

        def nc_block():
            def run(program):
                with nc.Block() as block:
                    program(block)
            return run

        def prepare():
            with ExitStack() as ctx:
                fill = sb(ctx, "fill", [1, 2, TAIL], I32)
                first_i = sb(ctx, "first_i", [1, GROUPS], I32)
                first = sb(ctx, "first", [1, GROUPS])
                bound = sb(ctx, "bound", [P, 1])
                part = sb(ctx, "part", [P, 1])
                before = sb(ctx, "before", [P, GROUPS])
                cnt = sb(ctx, "cnt", [P, 1])
                pos = sb(ctx, "pos", [P, 1])
                step = sb(ctx, "step", [P, TS])
                passed = sb(ctx, "passed", [P, TS])
                grp = sb(ctx, "grp", [1, TS])
                grp_c = sb(ctx, "grp_c", [1, TS])
                neg = sb(ctx, "neg", [1, TS])
                win = sb(ctx, "win", [1, TS])
                grp_col = sb(ctx, "grp_col", [P, TCH], I32)
                win_col = sb(ctx, "win_col", [P, TCH])
                eidx = sb(ctx, "eidx", [P, 2, TCH, GE], I32)
                rel = sb(ctx, "rel", [P, TCH, GE])
                inw = sb(ctx, "inw", [P, TCH, GE])
                off = sb(ctx, "off", [P, TCH, GE])
                idf = sb(ctx, "idf", [P, TCH, GE])
                ps_f = pb(ctx, "ps_f", [P, 512])
                ps_b = pb(ctx, "ps_b", [P, 512])
                ps_c = pb(ctx, "ps_c", [P, 512])
                ps_t = [pb(ctx, f"ps_t{k}", [P, 512]) for k in range(2)]

                filled, padded, got_first = sem("filled"), sem("padded"), sem("got_first")
                made, const = sem("made"), sem("const")
                first_f, first_b, counted = sem("first_f"), sem("first_b"), sem("counted")
                summed_b, table_row, cols_ps, cols_sb = sem("summed_b"), sem("table_row"), sem("cols_ps"), sem("cols_sb")
                rows_got, masked, turned, stored = sem("rows_got"), sem("masked"), sem("turned"), sem("stored")
                chain = sem("chain")

                @nc_block()
                def _(block):
                    @block.sync
                    def _(sp):
                        sp.dma_start(first_i[:, :], dst[:].rearrange("(a e) -> a e", a=1)[:, 0:E:GE],
                                     allow_slow_non_contiguous=True).then_inc(got_first, 16)
                        for pad, given in ((src_pad, src), (dst_pad, dst)):
                            flat = pad.rearrange("a b -> (a b)")
                            sp.dma_start(flat[0:E].rearrange("(a b) -> a b", a=16),
                                         given[:].rearrange("(a b) -> a b", a=16)).then_inc(padded, 16)
                        sp.wait_ge(filled, 2)
                        for k, pad in enumerate((src_pad, dst_pad)):
                            flat = pad.rearrange("a b -> (a b)")
                            sp.dma_start(flat[E:E + TAIL].rearrange("(a b) -> a b", a=1),
                                         fill[:, k, :]).then_inc(padded, 16)

                    @block.gpsimd
                    def _(pool):
                        nc.gpsimd.memset(fill[:, 0, :], 0).then_inc(filled, 1)
                        nc.gpsimd.memset(fill[:, 1, :], WINDOWS * P).then_inc(filled, 1)
                        nc.gpsimd.memset(ident[:, :], 0.0).then_inc(made, 1)
                        nc.gpsimd.memset(ones[:, :], 1.0).then_inc(const, 1)
                        exact = dict(allow_small_or_imprecise_dtypes=True)
                        nc.gpsimd.iota(bound[:, :], pattern=[[0, 1]], base=P, channel_multiplier=P, **exact).then_inc(const, 1)
                        nc.gpsimd.iota(part[:, :], pattern=[[0, 1]], base=0, channel_multiplier=1, **exact).then_inc(const, 1)
                        nc.gpsimd.iota(step[:, :], pattern=[[1, TS]], base=0, channel_multiplier=0, **exact).then_inc(const, 1)
                        nc.gpsimd.iota(lane[:, :], pattern=[[1, P]], base=0, channel_multiplier=0, **exact).then_inc(const, 1)
                        pool.wait_ge(made, 1)
                        nc.gpsimd.affine_select(out=ident[:, :], in_=ident[:, :], compare_op=ALU.not_equal, fill=1.0,
                                                base=0, pattern=[[-1, P]], channel_multiplier=1).then_inc(const, 1)
                        nc.gpsimd.memset(sums[:, :], 0.0).then_inc(made, 1)
                        pool.wait_ge(padded, 64)
                        pool.wait_ge(cols_sb, 1)
                        for c in range(TCH):
                            for k, pad in enumerate((src_pad, dst_pad)):
                                pool.indirect_dma_start(
                                    eidx[:, k, c, :], None, pad[:, :],
                                    bass.IndirectOffsetOnAxis(grp_col[:, c:c + 1], 0)).then_inc(rows_got, 16)
                        pool.wait_ge(made, 2)

                    @block.tensor
                    def _(pe):
                        pe.wait_ge(const, 6)
                        pe.wait_ge(first_f, 1)
                        nc.tensor.matmul(ps_f[:, 0:GROUPS], ones[0:1, :], first[0:1, :], start=True, stop=True).then_inc(first_b, 1)
                        pe.wait_ge(counted, 1)
                        nc.tensor.matmul(ps_b[:, 0:TS], ones[0:WINDOWS - 1, :], passed[0:WINDOWS - 1, :],
                                         start=True, stop=True).then_inc(summed_b, 1)
                        pe.wait_ge(table_row, 1)
                        for k, row in enumerate((grp_c, win)):
                            for c in range(TCH):
                                last = nc.tensor.matmul(ps_c[:, 2 * (k * TCH + c):2 * (k * TCH + c) + 1],
                                                        row[0:1, c * P:(c + 1) * P], ones[0:1, 0:1], start=True, stop=True)
                        last.then_inc(cols_ps, 1)
                        for n, (table, c) in enumerate((t, c) for t in range(2) for c in range(TCH)):
                            if n < TCH:
                                pe.wait_ge(masked, c + 1)
                            if n >= 2:
                                pe.wait_ge(stored, n - 1)
                            given = (rel, idf)[table][:, c, :]
                            for g in range(G):
                                last = nc.tensor.transpose(ps_t[n % 2][:, g * P:(g + 1) * P],
                                                           given[:, g * P:(g + 1) * P], ident[:, :])
                            last.then_inc(turned, 1)

                    @block.vector
                    def _(dve):
                        done = [0]

                        def then(ins):
                            done[0] += 1
                            ins.then_inc(chain, 1)
                            dve.wait_ge(chain, done[0])

                        dve.wait_ge(const, 6)
                        dve.wait_ge(got_first, 16)
                        nc.vector.tensor_copy(first[:, :], first_i[:, :]).then_inc(first_f, 1)
                        dve.wait_ge(first_b, 1)
                        then(nc.vector.tensor_scalar(before[:, :], ps_f[:, 0:GROUPS], bound[:, 0:1], None, ALU.is_lt))
                        then(nc.vector.tensor_reduce(cnt[:, :], before[:, :], AX, ALU.add))
                        then(nc.vector.tensor_tensor(pos[:, :], cnt[:, :], part[:, :], ALU.add))
                        nc.vector.tensor_scalar(passed[:, :], step[:, :], pos[:, 0:1], None, ALU.is_ge).then_inc(counted, 1)
                        dve.wait_ge(summed_b, 1)
                        then(nc.vector.tensor_tensor(grp[:, :], step[0:1, :], ps_b[0:1, 0:TS], ALU.subtract))
                        then(nc.vector.tensor_scalar(neg[:, :], grp[:, :], 0.0, None, ALU.is_lt))
                        then(nc.vector.tensor_tensor(win[:, :], ps_b[0:1, 0:TS], neg[:, :], ALU.subtract))
                        then(nc.vector.tensor_scalar(col_t[:, :], win[:, :], float(WIDTH), None, ALU.mult))
                        nc.vector.tensor_scalar(grp_c[:, :], grp[:, :], 0.0, float(GROUPS), ALU.max, ALU.min).then_inc(table_row, 1)
                        then(nc.vector.tensor_scalar(row_t[:, :], win[:, :], float(P), None, ALU.mult))
                        then(nc.vector.tensor_copy(qcol_t[:, :], win[:, :]))
                        then(nc.vector.tensor_scalar(qcol_t[:, :], qcol_t[:, :], QB - 1, None, ALU.bitwise_and))
                        then(nc.vector.tensor_scalar(qcol_t[:, :], qcol_t[:, :], float(2 * D), None, ALU.mult))
                        then(nc.vector.memset(new_t[:, 0:1], 1))
                        then(nc.vector.tensor_tensor(new_t[:, 1:TS], win[:, 1:TS], win[:, 0:TS - 1], ALU.not_equal))
                        dve.wait_ge(cols_ps, 1)
                        then(nc.vector.tensor_copy(grp_col[:, :], ps_c[:, 0:2 * TCH:2]))
                        then(nc.vector.tensor_scalar(win_col[:, :], ps_c[:, 2 * TCH:4 * TCH:2], float(P), None, ALU.mult))
                        dve.sem_inc(cols_sb, 1)

                        dve.wait_ge(rows_got, 16 * 2 * TCH)
                        for c in range(TCH):
                            then(nc.vector.tensor_scalar(rel[:, c, :], eidx[:, 1, c, :], win_col[:, c:c + 1], None, ALU.subtract))
                            then(nc.vector.tensor_scalar(inw[:, c, :], rel[:, c, :], 0.0, None, ALU.is_ge))
                            then(nc.vector.scalar_tensor_tensor(off[:, c, :], rel[:, c, :], float(P), inw[:, c, :],
                                                                ALU.is_lt, ALU.mult))
                            then(nc.vector.tensor_scalar(inw[:, c, :], off[:, c, :], -float(OUTSIDE), float(OUTSIDE),
                                                         ALU.mult, ALU.add))
                            nc.vector.tensor_tensor(idf[:, c, :], eidx[:, 0, c, :], inw[:, c, :], ALU.add).then_inc(masked, 1)
                        for n, (table, c) in enumerate((t, c) for t in range(2) for c in range(TCH)):
                            dve.wait_ge(turned, n + 1)
                            to = (rel_t, src_t)[table][:, c * P * G:(c + 1) * P * G]
                            nc.vector.tensor_copy(to.rearrange("p (s g) -> p g s", g=G),
                                                  ps_t[n % 2][:, 0:GE].rearrange("p (g s) -> p g s", g=G)).then_inc(stored, 1)

        def dense(layer, given, A_bc=None, C_bc=None):
            M = len(given)
            tag = str(layer)
            with ExitStack() as ctx:
                w_hi = sb(ctx, "w_hi" + tag, [P, M, KC, D], F32R)
                w_lo = sb(ctx, "w_lo" + tag, [P, M, KC, D], F32R)
                x_sb = sb(ctx, "x_sb" + tag, [P, 2, D])
                x1 = sb(ctx, "x1_sb", [P, 2, D]) if layer else x_sb
                h = sb(ctx, "h" + tag, [P, 2, D])
                st = sb(ctx, "st" + tag, [P, 6])
                mv = sb(ctx, "mv" + tag, [P, 2])
                sd = sb(ctx, "sd" + tag, [P, 1])
                rs = sb(ctx, "rs" + tag, [P, 2])
                nb = sb(ctx, "nb" + tag, [P, 2])
                hT_hi = sb(ctx, "hT_hi" + tag, [P, 2, D], F32R)
                hT_lo = sb(ctx, "hT_lo" + tag, [P, 2, D], F32R)
                o_sb = sb(ctx, "o_sb" + tag, [P, 2, 2, D])
                w_st = o_sb[:, :, :, :].rearrange("p a b d -> p (a b) d")
                if layer:
                    q_sb = sb(ctx, "q_sb", [P, 2, 2, D], F32R)
                else:
                    b_row = sb(ctx, "b_row", [1, D])
                    b_bc = sb(ctx, "b_bc", [P, D])
                ps_t = [pb(ctx, f"ps_t{tag}{k}", [P, 512]) for k in range(2)]
                ps_o = [[pb(ctx, f"ps_o{tag}{k}{j}", [P, 512]) for j in range(M)] for k in range(2)]

                w_in, w_turned, w_high, w_split, b_in = (sem(n + tag) for n in ("w_in", "w_turned", "w_high", "w_split", "b_in"))
                x_in, t_made, t_sum, normal = sems("x_in" + tag, 2), sem("t_made" + tag), sem("t_sum" + tag), sem("normal" + tag)
                var_ready, dev_ready, shift_ready, h_made = (sem(n + tag) for n in ("var_ready", "dev_ready", "shift_ready", "h_made"))
                q_high = sem("q_high" + tag)
                turned, high, split, made, by_act, by_dve = (
                    sem(n + tag) for n in ("turned", "high", "split", "made", "by_act", "by_dve"))
                kept, stored = sems("kept" + tag, 2), sems("stored" + tag, 2)

                def later(w):
                    return not isinstance(w, int) or w >= 2

                @nc_block()
                def _(block):
                    @block.sync
                    def _(sp):
                        def load(w, par, n=P):
                            if later(w):
                                sp.wait_ge(t_made if layer else h_made, w - 1)
                            sp.dma_start(x_sb[0:n, par, :], x[ds(w * P, n), :]).then_inc(x_in[par], 16)

                        def keep(w, par):
                            sp.wait_ge(h_made, w + 1)
                            sp.dma_start(x1_d[ds(w * P, P), :], x1[:, par, :]).then_inc(kept[par], 16)
                            sp.dma_start(h1_d[ds(w * P, P), :], h[:, par, :]).then_inc(kept[par], 16)

                        def store(w, par):
                            sp.wait_ge(by_act, w + 1)
                            sp.wait_ge(by_dve, w + 1)
                            rows = ds(w * P, P)
                            if layer:
                                sp.dma_start(q_d[rows, :], q_sb[:, par, :, :].rearrange("p a d -> p (a d)").bitcast(F32)).then_inc(stored[par], 16)
                                sp.dma_start(kv_d[rows, :], o_sb[:, par, :, :].rearrange("p a d -> p (a d)")).then_inc(stored[par], 16)
                            else:
                                sp.dma_start(y_d[rows, :], o_sb[:, par, 0, :]).then_inc(stored[par], 16)
                                sp.dma_start(z_d[rows, :], o_sb[:, par, 1, :]).then_inc(stored[par], 16)

                        def both(w, par, n=P):
                            load(w + 2, par, n)
                            if layer:
                                keep(w + 1, 1 - par)
                            store(w, par)

                        load(0, 0)
                        load(1, 1)
                        if not layer:
                            sp.dma_start(b_row[:, :], b_l[:].rearrange("(a n) -> a n", a=1)).then_inc(b_in, 16)
                        for k, w in enumerate(given):
                            if k:
                                sp.wait_ge(w_split, k * KC)
                            sp.dma_start(w_st, w[:, :].rearrange("(c p) i -> p c i", p=P)).then_inc(w_in, 16)
                        if layer:
                            keep(0, 0)
                        both(0, 0)
                        both(1, 1)
                        with sp.Fori(1, PAIRS - 1) as i:
                            for par in range(2):
                                both(2 * i + par, par)
                        both(WINDOWS - 3, 0, LAST)
                        if layer:
                            keep(WINDOWS - 1, 0)
                        store(WINDOWS - 2, 1)
                        store(WINDOWS - 1, 0)
                        for par in range(2):
                            if layer:
                                sp.wait_ge(kept[par], 32 * (PAIRS + 1 - par))
                            sp.wait_ge(stored[par], 32 * (PAIRS + 1 - par))

                    if layer:
                        @block.gpsimd
                        def _(pool):
                            def shift(w, i, par):
                                pool.wait_ge(x_in[par], 16 * (i + 1))
                                nc.gpsimd.tensor_tensor(x_sb[:, par, :], x_sb[:, par, :], C_bc[:, :], ALU.add).then_inc(t_sum, 1)

                            with pool.Fori(0, PAIRS) as i:
                                for par in range(2):
                                    shift(2 * i + par, i, par)
                            shift(WINDOWS - 1, PAIRS, 0)

                    @block.vector
                    def _(dve):
                        def part_low(n, source, lo, hi, of, count):
                            dve.wait_ge(of, n + 1)
                            nc.vector.tensor_tensor(lo, source, hi.bitcast(F32), ALU.subtract).then_inc(count, 1)

                        for k in range(M):
                            for c in range(KC):
                                n = k * KC + c
                                part_low(n, w_st[:, c, :] if layer else ps_o[n % 2][0][:, :],
                                         w_lo[:, k, c, :], w_hi[:, k, c, :], w_high, w_split)
                        if not layer:
                            dve.wait_ge(w_turned, M * KC + 1)
                            nc.vector.tensor_copy(b_bc[:, :], ps_o[0][1][:, :]).then_inc(w_split, 1)
                            dve.wait_ge(w_split, M * KC + 1)

                        def statistics(w, i, par):
                            at = w * 6

                            def then(ins, k):
                                ins.then_inc(normal, 1)
                                dve.wait_ge(normal, at + k)

                            if layer:
                                if later(w):
                                    dve.wait_ge(kept[par], 32 * i)
                                then(nc.vector.tensor_tensor(x1[:, par, :], window(w), A_bc[:, :], ALU.mult), 1)
                                dve.wait_ge(t_sum, w + 1)
                                then(nc.vector.tensor_tensor(x1[:, par, :], x1[:, par, :], x_sb[:, par, :], ALU.add), 2)
                                dve.sem_inc(t_made, 1)
                            else:
                                dve.wait_ge(x_in[par], 16 * (i + 1))
                                dve.sem_inc(normal, 2)
                            then(nc.vector.bn_stats(st[:, :], x1[:, par, :]), 3)
                            alone(dve)
                            then(nc.vector.bn_aggr(mv[:, :], st[:, :]), 4)
                            nc.vector.tensor_scalar(sd[:, :], mv[:, 1:2], EPS, None, ALU.add).then_inc(var_ready, 1)
                            dve.wait_ge(dev_ready, w + 1)
                            if later(w):
                                dve.wait_ge(h_made, w - 1)
                            then(nc.vector.reciprocal(rs[:, par:par + 1], sd[:, :]), 5)
                            then(nc.vector.scalar_tensor_tensor(nb[:, par:par + 1], mv[:, 0:1], -1.0, rs[:, par:par + 1],
                                                                ALU.mult, ALU.mult), 6)
                            dve.sem_inc(shift_ready, 1)

                        def split_h(w, par):
                            if later(w):
                                dve.wait_ge(made, M * (w - 1))
                            part_low(w, ps_t[par][:, :], hT_lo[:, par, :], hT_hi[:, par, :], high, split)

                        def read(w, i, par):
                            dve.wait_ge(made, M * w + 2)
                            if later(w):
                                dve.wait_ge(stored[par], 32 * i)
                            if layer:
                                nc.vector.tensor_copy(o_sb[:, par, 0, :], ps_o[par][1][:, :])
                                dve.wait_ge(q_high, w + 1)
                                nc.vector.scalar_tensor_tensor(q_sb[:, par, 1, :], ps_o[par][0][:, :], DH ** -0.5,
                                                               q_sb[:, par, 0, :].bitcast(F32), ALU.mult, ALU.subtract).then_inc(by_dve, 1)
                            else:
                                nc.vector.tensor_tensor(o_sb[:, par, 1, :], ps_o[par][1][:, :], b_bc[:, :], ALU.add).then_inc(by_dve, 1)

                        statistics(0, 0, 0)
                        statistics(1, 0, 1)
                        split_h(0, 0)
                        for w in range(2):
                            split_h(w + 1, 1 - w)
                            statistics(w + 2, 1, w)
                            read(w, 0, w)
                        with dve.Fori(1, PAIRS - 1) as i:
                            for par in range(2):
                                split_h(2 * i + par + 1, 1 - par)
                                statistics(2 * i + par + 2, i + 1, par)
                                read(2 * i + par, i, par)
                        for w in range(WINDOWS - 3, WINDOWS):
                            if w < WINDOWS - 1:
                                split_h(w + 1, 1 - w % 2)
                            if w < WINDOWS - 2:
                                statistics(w + 2, w // 2 + 1, w % 2)
                            read(w, w // 2, w % 2)

                    @block.scalar
                    def _(act):
                        for k in range(M):
                            for c in range(KC):
                                n = k * KC + c
                                if layer:
                                    act.wait_ge(w_in, 16 * (k + 1))
                                else:
                                    act.wait_ge(w_turned, n + 1)
                                nc.scalar.copy(w_hi[:, k, c, :], w_st[:, c, :] if layer else ps_o[n % 2][0][:, :]).then_inc(w_high, 1)

                        def norm(w, i, par):
                            act.wait_ge(var_ready, w + 1)
                            nc.scalar.activation(sd[:, :], sd[:, :], ACT.Sqrt).then_inc(dev_ready, 1)
                            act.wait_ge(shift_ready, w + 1)
                            if later(w):
                                if layer:
                                    act.wait_ge(kept[par], 32 * i)
                                act.wait_ge(turned, w - 1)
                            nc.scalar.activation(h[:, par, :], x1[:, par, :], ACT.Relu, bias=nb[:, par:par + 1],
                                                 scale=rs[:, par:par + 1]).then_inc(h_made, 1)

                        def high_h(w, par):
                            act.wait_ge(turned, w + 1)
                            if later(w):
                                act.wait_ge(made, M * (w - 1))
                            nc.scalar.copy(hT_hi[:, par, :], ps_t[par][:, :]).then_inc(high, 1)

                        def read(w, i, par):
                            act.wait_ge(made, M * w + M if layer else M * w + 1)
                            if later(w):
                                act.wait_ge(stored[par], 32 * i)
                            if layer:
                                nc.scalar.activation(q_sb[:, par, 0, :], ps_o[par][0][:, :], ACT.Copy, scale=DH ** -0.5).then_inc(q_high, 1)
                                nc.scalar.copy(o_sb[:, par, 1, :], ps_o[par][2][:, :]).then_inc(by_act, 1)
                            else:
                                nc.scalar.copy(o_sb[:, par, 0, :], ps_o[par][0][:, :]).then_inc(by_act, 1)

                        norm(0, 0, 0)
                        norm(1, 0, 1)
                        high_h(0, 0)
                        for w in range(2):
                            high_h(w + 1, 1 - w)
                            norm(w + 2, 1, w)
                            read(w, 0, w)
                        with act.Fori(1, PAIRS - 1) as i:
                            for par in range(2):
                                high_h(2 * i + par + 1, 1 - par)
                                norm(2 * i + par + 2, i + 1, par)
                                read(2 * i + par, i, par)
                        for w in range(WINDOWS - 3, WINDOWS):
                            if w < WINDOWS - 1:
                                high_h(w + 1, 1 - w % 2)
                            if w < WINDOWS - 2:
                                norm(w + 2, w // 2 + 1, w % 2)
                            read(w, w // 2, w % 2)

                    @block.tensor
                    def _(pe):
                        if not layer:
                            for k in range(M):
                                pe.wait_ge(w_in, 16 * (k + 1))
                                for c in range(KC):
                                    n = k * KC + c
                                    if n >= 2:
                                        pe.wait_ge(w_split, n - 1)
                                    for o in range(KC):
                                        last = nc.tensor.transpose(ps_o[n % 2][0][:, o * P:(o + 1) * P],
                                                                   w_st[:, o, c * P:(c + 1) * P], ident[:, :])
                                    last.then_inc(w_turned, 1)
                            pe.wait_ge(b_in, 16)
                            nc.tensor.matmul(ps_o[0][1][:, :], ones[0:1, :], b_row[0:1, :], start=True, stop=True).then_inc(w_turned, 1)

                        def turn(w, par):
                            pe.wait_ge(h_made, w + 1)
                            if later(w):
                                pe.wait_ge(split, w - 1)
                            for c in range(KC):
                                last = nc.tensor.transpose(ps_t[par][:, c * P:(c + 1) * P], h[:, par, c * P:(c + 1) * P], ident[:, :])
                            last.then_inc(turned, 1)

                        def products(w, par):
                            pe.wait_ge(split, w + 1)
                            if later(w):
                                pe.wait_ge(by_dve, w - 1)
                                pe.wait_ge(by_act, w - 1)
                            for k in range(M):
                                for c in range(KC):
                                    hi, lo = (t[:, par, c * P:(c + 1) * P] for t in (hT_hi, hT_lo))
                                    for j, (a, b) in enumerate(((hi, w_hi), (hi, w_lo), (lo, w_hi))):
                                        last = nc.tensor.matmul(ps_o[par][k][:, :], a, b[:, k, c, :],
                                                                start=(c == 0 and j == 0), stop=(c == KC - 1 and j == 2))
                                last.then_inc(made, 1)

                        turn(0, 0)
                        pe.wait_ge(w_split, M * KC + (0 if layer else 1))
                        for w in range(2):
                            turn(w + 1, 1 - w)
                            products(w, w)
                        with pe.Fori(1, PAIRS) as i:
                            for par in range(2):
                                turn(2 * i + par + 1, 1 - par)
                                products(2 * i + par, par)
                        products(WINDOWS - 1, 0)

        def aggregate():
            with ExitStack() as ctx:
                rows = sb(ctx, "rows", [P, U, G, D])
                hot = sb(ctx, "hot", [P, 4, G, P])
                idx = sb(ctx, "idx", [P, 2, H * G], I32)
                pss = [pb(ctx, f"pss{k}", [P, 1024]) for k in range(4)]
                cleared, staged, rows_in = sem("cleared"), sem("staged"), sems("rows_in", U)
                hot_made, ps_made, ps_free = sem("hot_made"), sem("ps_made"), sem("ps_free")

                @nc_block()
                def _(block):
                    @block.scalar
                    def _(act):
                        def stage(i, half):
                            nc.scalar.copy(idx[:, half, :], src_t[:, ds((i * U + half * H) * G, H * G)]).then_inc(staged, 1)

                        for half in range(2):
                            stage(0, half)
                        with act.Fori(0, ITERS) as i:
                            for half in range(2):
                                for u in range(half * H, half * H + H):
                                    act.wait_ge(rows_in[u], (i + 1) * 16 * G)
                                alone(act)
                                stage(i + 1, half)

                    @block.gpsimd
                    def _(pool):
                        limit = pool.alloc_register("limit0")
                        pool.reg_mov(limit, N - 1)
                        pool.wait_ge(cleared, 1)
                        with pool.Fori(0, ITERS) as i:
                            for u in range(U):
                                if u % H == 0:
                                    pool.wait_ge(staged, i * 2 + u // H + 1)
                                pool.wait_ge(ps_made, i * U + u + 1)
                                alone(pool)
                                for g in range(G):
                                    k = (u % H) * G + g
                                    pool.indirect_dma_start(rows[:, u, g, :], None, y_d[0:N, :],
                                                            bass.IndirectOffsetOnAxis(idx[:, u // H, k:k + 1], 0),
                                                            bounds_check=limit, oob_is_err=False).then_inc(rows_in[u], 16)

                    @block.vector
                    def _(dve):
                        nc.vector.memset(rows[:, :, :, :], 0.0).then_inc(cleared, 1)
                        dve.sem_inc(ps_free, 4)

                        def one_hot(i, u):
                            s = i * U + u
                            dve.wait_ge(ps_made, s + U - 3)
                            nc.vector.tensor_tensor(hot[:, u % 4, :, :], lane[:, :].unsqueeze(1).to_broadcast([P, G, P]),
                                                    rel_t[:, ds(s * G, G)].unsqueeze(2).to_broadcast([P, G, P]),
                                                    ALU.is_equal).then_inc(hot_made, 1)

                        def add(s, u, col):
                            dve.wait_ge(ps_made, s + U + 1)
                            dve.wait_ge(ps_free, s + 4)
                            to = sums[:, ds(col, D + 1)]
                            nc.vector.tensor_tensor(to, to, pss[u % 4][:, 0:D + 1], ALU.add).then_inc(ps_free, 1)

                        cols = load_values(mybir.EngineType.DVE, col_t, 0, U, (WINDOWS - 1) * WIDTH)
                        for u in range(U):
                            one_hot(0, u)
                            if u >= 2:
                                add(u - 2, u - 2, cols[u - 2])
                        with dve.Fori(1, ITERS) as i:
                            cols = load_values(mybir.EngineType.DVE, col_t, i * U - 2, U, (WINDOWS - 1) * WIDTH)
                            for u in range(U):
                                one_hot(i, u)
                                add(i * U + u - 2, u + 2, cols[u])
                        cols = load_values(mybir.EngineType.DVE, col_t, STEPS - 2, 2, (WINDOWS - 1) * WIDTH)
                        for k in range(2):
                            add(STEPS - 2 + k, U - 2 + k, cols[k])

                    @block.tensor
                    def _(pe):
                        pe.sem_inc(ps_made, U)
                        with pe.Fori(0, ITERS) as i:
                            for u in range(U):
                                s = i * U + u
                                ps = pss[u % 4]
                                pe.wait_ge(hot_made, s + 1)
                                pe.wait_ge(ps_free, s + 1)
                                for g in range(G):
                                    last = nc.tensor.matmul(ps[:, D:D + 2], hot[:, u % 4, g, :], ones[:, 0:2],
                                                            start=(g == 0), stop=(g == G - 1))
                                pe.wait_ge(rows_in[u], (i + 1) * 16 * G)
                                for g in range(G):
                                    last = nc.tensor.matmul(ps[:, 0:D], hot[:, u % 4, g, :], rows[:, u, g, :],
                                                            start=(g == 0), stop=(g == G - 1))
                                last.then_inc(ps_made, 1)

        def load_values(engine, table, s, n, most):
            _, values = nc.values_load_multi_w_load_instructions(
                table[0:1, ds(s, n)], engines=[engine], min_val=0, max_val=most,
                skip_runtime_bounds_check_because="a step's window is one of 0..WINDOWS-1 by how the tables are made")
            return values

        def combine(S1, S2):
            with ExitStack() as ctx:
                z = sb(ctx, "z_sb", [P, 2, D])
                rd = sb(ctx, "rd", [P, WINDOWS])
                sq = sb(ctx, "sq", [P, 2, D])
                z_in, degrees, added_z, rect, squared, zero1, zero2, summed1, summed2 = (
                    sems("z_in", 2), sem("degrees"), sem("added_z"), sem("rect"), sem("squared"), sem("zero1"), sem("zero2"),
                    sem("summed1"), sem("summed2"))

                @nc_block()
                def _(block):
                    @block.sync
                    def _(sp):
                        def load(w, par):
                            sp.wait_ge(added_z, w + 1)
                            sp.dma_start(z[:, par, :], z_d[ds(w * P, P), :]).then_inc(z_in[par], 16)

                        with sp.Fori(0, PAIRS) as i:
                            for par in range(2):
                                load(2 * i + par, par)
                        load(WINDOWS - 1, 0)

                    @block.vector
                    def _(dve):
                        nc.vector.memset(S1[:, :], 0.0).then_inc(zero1, 1)
                        degree = sums[:, :].rearrange("p (w c) -> p w c", c=WIDTH)[:, :, D]
                        nc.vector.tensor_scalar(rd[:, :], degree, 1.0, None, ALU.max).then_inc(degrees, 1)
                        dve.wait_ge(degrees, 1)
                        nc.vector.reciprocal(rd[:, :], rd[:, :]).then_inc(degrees, 1)
                        dve.wait_ge(degrees, 2)
                        dve.wait_ge(zero1, 1)
                        spread = sums[:, :].rearrange("p (w c) -> p w c", c=WIDTH)[:, :, D + 1]
                        nc.vector.tensor_copy(spread, rd[:, :]).then_inc(degrees, 1)
                        dve.wait_ge(degrees, 3)
                        dve.sem_inc(added_z, 2)

                        def add_z(w, i, par):
                            dve.wait_ge(z_in[par], 16 * (i + 1))
                            alone(dve)
                            nc.vector.scalar_tensor_tensor(window(w), window(w), sums[:, ds(w * WIDTH + D + 1, 1)], z[:, par, :],
                                                           ALU.mult, ALU.add).then_inc(added_z, 1)

                        def add_h(w, n=P):
                            dve.wait_ge(rect, w + 1)
                            nc.vector.tensor_tensor(S1[0:n, :], S1[0:n, :], window(w)[0:n, :], ALU.add).then_inc(summed1, 1)
                            dve.wait_ge(summed1, w + 1)

                        add_z(0, 0, 0)
                        with dve.Fori(0, PAIRS) as i:
                            for par in range(2):
                                add_z(2 * i + par + 1, i + par, 1 - par)
                                add_h(2 * i + par)
                        add_h(WINDOWS - 1, LAST)

                    @block.scalar
                    def _(act):
                        def rectify(w, i, par):
                            act.wait_ge(added_z, w + 3)
                            alone(act)
                            nc.scalar.activation(window(w), window(w), ACT.Relu).then_inc(rect, 1)
                            act.wait_ge(rect, w + 1)
                            if not isinstance(i, int) or i:
                                act.wait_ge(summed2, w - 1)
                            alone(act)
                            nc.scalar.activation(sq[:, par, :], window(w), ACT.Square).then_inc(squared, 1)

                        rectify(0, 0, 0)
                        rectify(1, 0, 1)
                        with act.Fori(1, PAIRS) as i:
                            for par in range(2):
                                rectify(2 * i + par, i, par)
                        rectify(WINDOWS - 1, PAIRS, 0)

                    @block.gpsimd
                    def _(pool):
                        nc.gpsimd.memset(S2[:, :], 0.0).then_inc(zero2, 1)
                        pool.wait_ge(zero2, 1)

                        def add_square(w, par, n=P):
                            pool.wait_ge(squared, w + 1)
                            nc.gpsimd.tensor_tensor(S2[0:n, :], S2[0:n, :], sq[0:n, par, :], ALU.add).then_inc(summed2, 1)
                            pool.wait_ge(summed2, w + 1)

                        with pool.Fori(0, PAIRS) as i:
                            for par in range(2):
                                add_square(2 * i + par, par)
                        add_square(WINDOWS - 1, 0, LAST)

        def batch_norm(tag, before, gamma, beta, after):
            with ExitStack() as ctx:
                A_bc = sb(ctx, "A_bc" + tag, [P, D])
                C_bc = sb(ctx, "C_bc" + tag, [P, D])
                with ExitStack() as inner:
                    S1 = sb(inner, "S1" + tag, [P, D])
                    S2 = sb(inner, "S2" + tag, [P, D])
                    before(S1, S2)
                    coefficients(tag, gamma, beta, S1, S2, A_bc, C_bc)
                after(A_bc, C_bc)

        def coefficients(tag, gamma, beta, S1, S2, A_bc, C_bc):
            with ExitStack() as ctx:
                gb = sb(ctx, "gb" + tag, [1, 2, D])
                mu = sb(ctx, "mu" + tag, [P, D])
                var = sb(ctx, "var" + tag, [P, D])
                ps_s = [pb(ctx, f"ps_s{tag}{k}", [P, 512]) for k in range(4)]
                gb_in, tot, chain, var_ready, dev_ready = (sem(n + tag) for n in ("gb_in", "tot", "cchain", "bn_var", "bn_dev"))

                @nc_block()
                def _(block):
                    @block.sync
                    def _(sp):
                        for k, v in enumerate((gamma, beta)):
                            sp.dma_start(gb[:, k, :], v[:].rearrange("(a n) -> a n", a=1)).then_inc(gb_in, 16)

                    @block.tensor
                    def _(pe):
                        nc.tensor.matmul(ps_s[0][:, :], ones[:, :], S1[:, :], start=True, stop=True).then_inc(tot, 1)
                        nc.tensor.matmul(ps_s[1][:, :], ones[:, :], S2[:, :], start=True, stop=True).then_inc(tot, 1)
                        pe.wait_ge(gb_in, 32)
                        for k in range(2):
                            nc.tensor.matmul(ps_s[2 + k][:, :], ones[0:1, :], gb[0:1, k, :], start=True, stop=True).then_inc(tot, 1)

                    @block.vector
                    def _(dve):
                        done = [0]

                        def then(ins):
                            done[0] += 1
                            ins.then_inc(chain, 1)
                            dve.wait_ge(chain, done[0])

                        dve.wait_ge(tot, 1)
                        then(nc.vector.tensor_scalar(mu[:, :], ps_s[0][:, :], 1.0 / N, None, ALU.mult))
                        then(nc.vector.tensor_tensor(var[:, :], mu[:, :], mu[:, :], ALU.mult))
                        dve.wait_ge(tot, 2)
                        then(nc.vector.scalar_tensor_tensor(var[:, :], ps_s[1][:, :], 1.0 / N, var[:, :], ALU.mult, ALU.subtract))
                        nc.vector.tensor_scalar(var[:, :], var[:, :], 0.0, EPS, ALU.max, ALU.add).then_inc(var_ready, 1)
                        dve.wait_ge(dev_ready, 1)
                        then(nc.vector.reciprocal(var[:, :], var[:, :]))
                        dve.wait_ge(tot, 4)
                        then(nc.vector.tensor_tensor(A_bc[:, :], ps_s[2][:, :], var[:, :], ALU.mult))
                        then(nc.vector.tensor_tensor(mu[:, :], mu[:, :], A_bc[:, :], ALU.mult))
                        then(nc.vector.tensor_tensor(C_bc[:, :], ps_s[3][:, :], mu[:, :], ALU.subtract))

                    @block.scalar
                    def _(act):
                        act.wait_ge(var_ready, 1)
                        nc.scalar.activation(var[:, :], var[:, :], ACT.Sqrt).then_inc(dev_ready, 1)

        def attend():
            HA = 6
            with ExitStack() as ctx:
                kv = sb(ctx, "kv", [P, U, G, 2 * D])
                q = sb(ctx, "q", [P, QB * 2 * D], F32R)
                hot = sb(ctx, "hot1", [P, U, G, P])
                hotT = sb(ctx, "hotT", [P, 2, G * P], F32R)
                score = sb(ctx, "score", [P, U, G * HEADS])
                wgt = sb(ctx, "wgt", [P, U, G * HEADS])
                idx = sb(ctx, "idx1", [P, 2, H * G], I32)
                ps_q = [pb(ctx, f"ps_q{k}", [P, 512]) for k in range(G)]
                ps_h = pb(ctx, "ps_h", [P, 512])
                pss = [pb(ctx, f"psa{k}", [P, 1024]) for k in range(2)]
                cleared, zeroed, staged, rows_in, q_in = sem("cleared1"), sem("zeroed1"), sem("staged1"), sems("rows_in1_", U), sems("q_in", QB)
                hot_made, turned, copied, expanded, multiplied = (
                    sem("hot_made1"), sem("hot_turned"), sem("hot_copied"), sem("expanded"), sem("multiplied"))
                reduced, clipped, weighed, by_act, by_dve = (
                    sem("reduced"), sem("clipped"), sem("weighed"), sem("scaled_by_act"), sem("scaled_by_dve"))
                ps_made, ps_free = sem("ps_made1"), sem("ps_free1")

                def steps(i, u, delta):
                    s = i * U + u + delta
                    if isinstance(i, int) and not 0 <= s < STEPS:
                        return None
                    return s, i + (u + delta) // U, (u + delta) % U

                @nc_block()
                def _(block):
                    def times(eng, at, first, last, held):
                        for t in range(first, 0):
                            at(-1, t + U, held(t, t + 1))
                        regs = held(0, U)
                        for u in range(U):
                            at(0, u, regs)
                        with eng.Fori(1, ITERS - 1) as i:
                            regs = held(i * U, None)
                            for u in range(U):
                                at(i, u, regs)
                        regs = held(STEPS - U, STEPS)
                        for u in range(U):
                            at(ITERS - 1, u, regs)
                        for t in range(STEPS, STEPS + last):
                            at(ITERS, t - STEPS, held(t, t + 1))

                    def no_registers(t0, t1):
                        return None

                    def registers(engine, table, lead, most):
                        def held(t0, t1):
                            if t1 is None:
                                vals = load_values(engine, table, t0 + lead, U, most)
                                return lambda u: vals[u]
                            a, b = max(t0 + lead, 0), min(t1 + lead, STEPS)
                            if a >= b:
                                return None
                            vals = load_values(engine, table, a, b - a, most)
                            return lambda u: vals[u - (a - lead) % U]
                        return held

                    @block.sync
                    def _(sp):
                        def fetch(i, u, regs):
                            s, r = i * U + u, u % QB
                            row, col, new = regs
                            sp.wait_ge(expanded, s * G + G)
                            sp.dma_start(q[:, ds(col[u], 2 * D)].bitcast(F32), q_d[ds(row[u], P), :], cond=new[u]).then_inc(q_in[r], 16)

                        with sp.Fori(0, ITERS) as i:
                            regs = [load_values(mybir.EngineType.SP, table, i * U, U, most) for table, most in
                                    ((row_t, (WINDOWS - 1) * P), (qcol_t, (QB - 1) * 2 * D), (new_t, 1))]
                            for u in range(U):
                                fetch(i, u, regs)

                    @block.gpsimd
                    def _(pool):
                        limit = pool.alloc_register("limit1")
                        pool.reg_mov(limit, N - 1)
                        pool.wait_ge(cleared, 1)
                        with pool.Fori(0, ITERS) as i:
                            for u in range(U):
                                if u % H == 0:
                                    pool.wait_ge(staged, i * 2 + u // H + 1)
                                pool.wait_ge(ps_made, i * U + u + 1)
                                alone(pool)
                                for g in range(G):
                                    k = (u % H) * G + g
                                    pool.indirect_dma_start(kv[:, u, g, :], None, kv_d[0:N, :],
                                                            bass.IndirectOffsetOnAxis(idx[:, u // H, k:k + 1], 0),
                                                            bounds_check=limit, oob_is_err=False).then_inc(rows_in[u], 16)

                    @block.scalar
                    def _(act):
                        act.sem_inc(copied, 1)

                        def stage(i, half):
                            nc.scalar.copy(idx[:, half, :], src_t[:, ds((i * U + half * H) * G, H * G)]).then_inc(staged, 1)

                        def copy_hot(s, i, u):
                            act.wait_ge(turned, s + 1)
                            act.wait_ge(expanded, G * s + 3 * G)
                            nc.scalar.copy(hotT[:, u % 2, :], ps_h[:, 0:G * P]).then_inc(copied, 1)

                        def weigh(s, i, u):
                            act.wait_ge(clipped, s + 1)
                            nc.scalar.activation(wgt[:, u, :], score[:, u, :], ACT.Exp).then_inc(weighed, 1)
                            act.wait_ge(weighed, s + 1)
                            for g in range(G):
                                for h in range(HA):
                                    v = kv[:, u, g, D + h * DH:D + (h + 1) * DH]
                                    last = nc.scalar.mul(v, v, wgt[:, u, g * HEADS + h:g * HEADS + h + 1])
                            last.then_inc(by_act, 1)

                        def restage(i, half):
                            for u in range(half * H, half * H + H):
                                act.wait_ge(rows_in[u], 16 * G * (i + 1))
                            alone(act)
                            stage(i + 1, half)

                        def at(i, u, regs):
                            if step := steps(i, u, -1):
                                weigh(*step)
                            if u == H and (not isinstance(i, int) or 0 <= i < ITERS):
                                restage(i, 0)
                            if u == 0 and (not isinstance(i, int) or 0 < i < ITERS):
                                restage(i - 1, 1)
                            if step := steps(i, u, 2):
                                copy_hot(*step)

                        for half in range(2):
                            stage(0, half)
                        times(act, at, -2, 1, no_registers)

                    @block.vector
                    def _(dve):
                        nc.vector.memset(kv[:, :, :, :], 0.0).then_inc(cleared, 1)
                        nc.vector.memset(sums[:, :], 0.0).then_inc(zeroed, 1)
                        dve.wait_ge(zeroed, 1)
                        dve.sem_inc(ps_free, 2)
                        dve.sem_inc(multiplied, G)

                        def one_hot(s, i, u):
                            dve.wait_ge(ps_made, s + 1)
                            nc.vector.tensor_tensor(hot[:, u, :, :], lane[:, :].unsqueeze(1).to_broadcast([P, G, P]),
                                                    rel_t[:, ds(s * G, G)].unsqueeze(2).to_broadcast([P, G, P]),
                                                    ALU.is_equal).then_inc(hot_made, 1)

                        def multiply(s, i, u):
                            dve.wait_ge(rows_in[u], 16 * G * (i + 1))
                            for g in range(G):
                                dve.wait_ge(expanded, (QB + s) * G + g + 1)
                                k = kv[:, u, g, 0:D]
                                nc.vector.tensor_tensor(k, k, ps_q[g][:, :], ALU.mult).then_inc(multiplied, 1)

                        def scale(s, i, u):
                            dve.wait_ge(weighed, s + 1)
                            v = kv[:, u, :, D + HA * DH:2 * D].rearrange("p g (h d) -> p g h d", d=DH)
                            w = wgt[:, u, :].rearrange("p (g h) -> p g h", g=G)[:, :, HA:HEADS]
                            nc.vector.tensor_tensor(v, v, w.unsqueeze(3).to_broadcast([P, G, HEADS - HA, DH]), ALU.mult).then_inc(by_dve, 1)

                        def reduce(s, i, u):
                            dve.wait_ge(multiplied, G * s + 2 * G)
                            nc.vector.tensor_reduce(score[:, u, :].rearrange("p (g h) -> p g h", g=G),
                                                    kv[:, u, :, 0:D].rearrange("p g (h d) -> p g h d", h=HEADS),
                                                    AX, ALU.add).then_inc(reduced, 1)

                        def clip(s, i, u):
                            dve.wait_ge(reduced, s + 1)
                            nc.vector.tensor_scalar(score[:, u, :], score[:, u, :], -5.0, 5.0, ALU.max, ALU.min).then_inc(clipped, 1)

                        def add(s, i, u, col):
                            dve.wait_ge(ps_made, s + U + 1)
                            dve.wait_ge(ps_free, s + 2)
                            to = sums[:, ds(col, WIDTH)]
                            nc.vector.tensor_tensor(to, to, pss[u % 2][:, 0:WIDTH], ALU.add).then_inc(ps_free, 1)

                        def at(i, u, col):
                            if step := steps(i, u, 0):
                                multiply(*step)
                            if step := steps(i, u, -1):
                                scale(*step)
                            if step := steps(i, u, 0):
                                reduce(*step)
                            if step := steps(i, u, -2):
                                add(*step, col(u))
                            if step := steps(i, u, 0):
                                clip(*step)
                            if step := steps(i, u, 3):
                                one_hot(*step)

                        times(dve, at, -3, 2, registers(mybir.EngineType.DVE, col_t, -2, (WINDOWS - 1) * WIDTH))

                    @block.tensor
                    def _(pe):
                        pe.sem_inc(ps_made, U)
                        pe.sem_inc(expanded, G * QB)

                        def turn(s, i, u):
                            pe.wait_ge(hot_made, s + 1)
                            pe.wait_ge(copied, s + 1)
                            for g in range(G):
                                last = nc.tensor.transpose(ps_h[:, g * P:(g + 1) * P], hot[:, u, g, :], ident[:, :])
                            last.then_inc(turned, 1)

                        def expand(s, i, u, col):
                            pe.wait_ge(copied, s + 2)
                            pe.wait_ge(q_in[u % QB], 16 * (i * (U // QB) + u // QB + 1))
                            for g in range(G):
                                pe.wait_ge(multiplied, G * s + g + 1)
                                for k in range(2):
                                    last = nc.tensor.matmul(ps_q[g][:, :], hotT[:, u % 2, g * P:(g + 1) * P],
                                                            q[:, ds(col + k * D, D)], start=(k == 0), stop=(k == 1))
                                last.then_inc(expanded, 1)

                        def total(s, i, u):
                            ps = pss[u % 2]
                            pe.wait_ge(ps_free, s + 1)
                            pe.wait_ge(weighed, s + 1)
                            for g in range(G):
                                nc.tensor.matmul(ps[:, D:WIDTH], hot[:, u, g, :], wgt[:, u, g * HEADS:(g + 1) * HEADS],
                                                 start=(g == 0), stop=(g == G - 1))
                            pe.wait_ge(by_act, s + 1)
                            pe.wait_ge(by_dve, s + 1)
                            for g in range(G):
                                last = nc.tensor.matmul(ps[:, 0:D], hot[:, u, g, :], kv[:, u, g, D:2 * D],
                                                        start=(g == 0), stop=(g == G - 1))
                            last.then_inc(ps_made, 1)

                        def at(i, u, col):
                            if step := steps(i, u, -2):
                                total(*step)
                            if step := steps(i, u, 2):
                                turn(*step)
                            if step := steps(i, u, 1):
                                expand(*step, col(u))

                        times(pe, at, -2, 2, registers(mybir.EngineType.PE, qcol_t, 1, (QB - 1) * 2 * D))

        def attended(S1, S2):
            with ExitStack() as ctx:
                h1 = sb(ctx, "h1b", [P, 2, D])
                zr = sb(ctx, "zr", [P, 2, HEADS])
                sq = sb(ctx, "sq1", [P, 2, D])
                zeroed1, zeroed2, h_in, chain, made, squared, added = (
                    sem("zeroed_S1"), sem("zeroed_S2"), sems("h_in2", 2), sem("achain"), sem("h_made"), sem("squared1"), sem("added1"))

                @nc_block()
                def _(block):
                    @block.sync
                    def _(sp):
                        def load(w, par, n=P):
                            sp.wait_ge(made, w + 1)
                            sp.dma_start(h1[0:n, par, :], h1_d[ds(w * P, n), :]).then_inc(h_in[par], 16)

                        with sp.Fori(0, PAIRS) as i:
                            for par in range(2):
                                load(2 * i + par, par)
                        load(WINDOWS - 1, 0)

                    @block.gpsimd
                    def _(pool):
                        nc.gpsimd.memset(S2[:, :], 0.0).then_inc(zeroed2, 1)
                        pool.wait_ge(zeroed2, 1)

                        def add(w, par, n=P):
                            pool.wait_ge(squared, w + 1)
                            nc.gpsimd.tensor_tensor(S2[0:n, :], S2[0:n, :], sq[0:n, par, :], ALU.add).then_inc(added, 1)
                            pool.wait_ge(added, w + 1)

                        with pool.Fori(0, PAIRS) as i:
                            for par in range(2):
                                add(2 * i + par, par)
                        add(WINDOWS - 1, 0, LAST)

                    @block.scalar
                    def _(act):
                        def square(w, par):
                            act.wait_ge(made, w + 3)
                            if not isinstance(w, int) or w >= 2:
                                act.wait_ge(added, w - 1)
                            alone(act)
                            nc.scalar.activation(sq[:, par, :], window(w), ACT.Square).then_inc(squared, 1)

                        square(0, 0)
                        square(1, 1)
                        with act.Fori(1, PAIRS) as i:
                            for par in range(2):
                                square(2 * i + par, par)
                        square(WINDOWS - 1, 0)

                    @block.vector
                    def _(dve):
                        dve.sem_inc(made, 2)
                        nc.vector.memset(S1[:, :], 0.0).then_inc(zeroed1, 1)
                        dve.wait_ge(zeroed1, 1)
                        K = 5

                        def combine(w, i, par, n=P):
                            def then(ins, k):
                                ins.then_inc(chain, 1)
                                dve.wait_ge(chain, w * K + k)

                            then(nc.vector.tensor_scalar(zr[:, par, :], sums[:, ds(w * WIDTH + D, HEADS)], 1e-6, None, ALU.add), 1)
                            then(nc.vector.reciprocal(zr[:, par, :], zr[:, par, :]), 2)
                            v = window(w).rearrange("p (h d) -> p h d", h=HEADS)
                            then(nc.vector.tensor_tensor(v, v, zr[:, par, :].unsqueeze(2).to_broadcast([P, HEADS, DH]), ALU.mult), 3)
                            dve.wait_ge(h_in[par], 16 * (i + 1))
                            then(nc.vector.tensor_tensor(window(w), window(w), h1[:, par, :], ALU.add), 4)
                            dve.sem_inc(made, 1)
                            then(nc.vector.tensor_tensor(S1[0:n, :], S1[0:n, :], window(w)[0:n, :], ALU.add), 5)

                        with dve.Fori(0, PAIRS) as i:
                            for par in range(2):
                                combine(2 * i + par, i, par)
                        combine(WINDOWS - 1, PAIRS, 0, LAST)

        def finish(A_bc, C_bc):
            with ExitStack() as ctx:
                x1 = sb(ctx, "x1b", [P, 2, D])
                o = sb(ctx, "o", [P, 2, D])
                x_in, shifted, scaled, done, stored = sems("x_in3", 2), sem("shifted"), sem("scaled1"), sem("done"), sems("stored_", 2)

                @nc_block()
                def _(block):
                    @block.sync
                    def _(sp):
                        def load(w, par):
                            sp.wait_ge(done, w + 1)
                            sp.dma_start(x1[:, par, :], x1_d[ds(w * P, P), :]).then_inc(x_in[par], 16)

                        with sp.Fori(0, PAIRS) as i:
                            for par in range(2):
                                load(2 * i + par, par)
                        load(WINDOWS - 1, 0)

                    @block.scalar
                    def _(act):
                        def store(w, par, n=P):
                            act.wait_ge(done, w + 3)
                            act.dma_start(out[ds(w * P, n), :], o[0:n, par, :]).then_inc(stored[par], 16)

                        with act.Fori(0, PAIRS) as i:
                            for par in range(2):
                                store(2 * i + par, par)
                        store(WINDOWS - 1, 0, LAST)
                        for par in range(2):
                            act.wait_ge(stored[par], 16 * (PAIRS + 1 - par))

                    @block.gpsimd
                    def _(pool):
                        def shift(w, i, par):
                            pool.wait_ge(x_in[par], 16 * (i + 1))
                            nc.gpsimd.tensor_tensor(x1[:, par, :], x1[:, par, :], C_bc[:, :], ALU.add).then_inc(shifted, 1)

                        with pool.Fori(0, PAIRS) as i:
                            for par in range(2):
                                shift(2 * i + par, i, par)
                        shift(WINDOWS - 1, PAIRS, 0)

                    @block.vector
                    def _(dve):
                        dve.sem_inc(done, 2)

                        def scale(w):
                            nc.vector.tensor_tensor(window(w), window(w), A_bc[:, :], ALU.mult).then_inc(scaled, 1)

                        def add(w, i, par):
                            dve.wait_ge(shifted, w + 1)
                            dve.wait_ge(scaled, w + 1)
                            if not isinstance(i, int) or i:
                                dve.wait_ge(stored[par], 16 * i)
                            nc.vector.tensor_tensor(o[:, par, :], window(w), x1[:, par, :], ALU.add).then_inc(done, 1)

                        scale(0)
                        for w in range(2):
                            scale(w + 1)
                            add(w, 0, w)
                        with dve.Fori(1, PAIRS) as i:
                            for par in range(2):
                                scale(2 * i + par + 1)
                                add(2 * i + par, i, par)
                        add(WINDOWS - 1, PAIRS, 0)

        prepare()
        dense(0, (W_l, W_r))
        aggregate()
        batch_norm("0", combine, gamma0, beta0, lambda A, C: dense(1, (Wq, Wk, Wv), A, C))
        attend()
        batch_norm("1", attended, gamma1, beta1, finish)


def kernel(**inputs):
    import numpy as np
    import concourse.bacc as bacc
    from concourse.bass_utils import run_bass_kernel_spmd

    names = ["x", "src", "dst", "L0_gnn_W_l", "L0_gnn_b_l", "L0_gnn_W_r", "L0_gnn_gamma", "L0_gnn_beta",
             "L1_gnn_Wq", "L1_gnn_Wk", "L1_gnn_Wv", "L1_gnn_bn_gamma", "L1_gnn_bn_beta"]
    nc = bacc.Bacc("TRN2", target_bir_lowering=False, num_devices=1)
    arrays, args = {}, []
    for name in names:
        a = np.ascontiguousarray(inputs[name])
        arrays["in_" + name] = a
        args.append(nc.dram_tensor("in_" + name, a.shape, mybir.dt.from_np(a.dtype), kind="ExternalInput").ap())
    shape = inputs["x"].shape
    result = nc.dram_tensor("result", shape, F32, kind="ExternalOutput").ap()
    build(nc, *args, result)
    r = run_bass_kernel_spmd(nc, [arrays], core_ids=[0])
    return r.results[0]["result"]
```

```python
from contextlib import ExitStack

import concourse.bass as bass
from concourse import mybir

F32 = mybir.dt.float32
F32R = mybir.dt.float32r
I32 = mybir.dt.int32
I16 = mybir.dt.int16
ALU = mybir.AluOpType
ACT = mybir.ActivationFunctionType
AX = mybir.AxisListType.X
ds = bass.ds

P = 128
EPS = 1e-5
HEADS = 8


def build(nc, x, src, dst, W_l, b_l, W_r, gamma0, beta0, Wq, Wk, Wv, gamma1, beta1, out):
    N, D = x.shape
    E = src.shape[0]
    DH = D // HEADS
    KC = D // P
    WINDOWS = -(-N // P)
    LAST = N - (WINDOWS - 1) * P
    WIDTH = D + HEADS
    G = 2
    GE = G * P
    GROUPS = -(-E // GE)
    U = 8
    H = 2
    ITERS = -(-(GROUPS + WINDOWS - 1) // U)
    STEPS = ITERS * U
    TCH = -(-(STEPS + U) // P)
    TS = TCH * P
    TAIL = (GROUPS + 1) * GE - E
    OUTSIDE = 1 << 14
    PAIRS = WINDOWS // 2
    NB = 4
    FOURS = WINDOWS // NB
    QB = 4
    assert WINDOWS * WIDTH < 1 << 15 and N <= OUTSIDE and WINDOWS == 2 * PAIRS + 1 == NB * FOURS + 1 and TS <= 512 and GROUPS <= 512 and D == 512

    src_pad = nc.dram_tensor("src_pad", (GROUPS + 1, GE), I32).ap()
    dst_pad = nc.dram_tensor("dst_pad", (GROUPS + 1, GE), I32).ap()
    y_d = nc.dram_tensor("y_d", (WINDOWS * P, D), F32).ap()
    z_d = nc.dram_tensor("z_d", (WINDOWS * P, D), F32).ap()
    h1_d = nc.dram_tensor("h1_d", (WINDOWS * P, D), F32).ap()
    x1_d = nc.dram_tensor("x1_d", (WINDOWS * P, D), F32).ap()
    kv_d = nc.dram_tensor("kv_d", (WINDOWS * P, 2 * D), F32).ap()
    q_d = nc.dram_tensor("q_d", (WINDOWS * P, 2 * D), F32).ap()

    def sb(ctx, name, shape, dt=F32):
        return ctx.enter_context(nc.sbuf_tensor(name, shape, dt))

    def pb(ctx, name, shape):
        return ctx.enter_context(nc.psum_tensor(name, shape, F32))

    life = ExitStack()

    def sem(name):
        return life.enter_context(nc.semaphore(name))

    def sems(name, n):
        return [sem(f"{name}{k}") for k in range(n)]

    with life:
        sums = sb(life, "sums", [P, WINDOWS * WIDTH])
        src_t = sb(life, "src_t", [P, TS * G], I32)
        rel_t = sb(life, "rel_t", [P, TS * G])
        col_t = sb(life, "col_t", [1, TS], I16)
        row_t = sb(life, "row_t", [1, TS], I16)
        qcol_t = sb(life, "qcol_t", [1, TS], I16)
        par_t = sb(life, "par_t", [1, TS], I16)
        new_t = sb(life, "new_t", [1, TS], I16)
        zero = sb(life, "zero", [1, D], F32R)
        ident = sb(life, "ident", [P, P])
        ones = sb(life, "ones", [P, P])
        lane = sb(life, "lane", [P, P])

        alone_count = sem("alone_count")

        def alone(eng):
            eng.sem_inc(alone_count, 1)

        def window(w, width=D):
            return sums[:, ds(w * WIDTH, width)]

        def nc_block():
            def run(program):
                with nc.Block() as block:
                    program(block)
            return run

        def prepare():
            with ExitStack() as ctx:
                fill = sb(ctx, "fill", [1, 2, TAIL], I32)
                first_i = sb(ctx, "first_i", [1, GROUPS], I32)
                first = sb(ctx, "first", [1, GROUPS])
                bound = sb(ctx, "bound", [P, 1])
                part = sb(ctx, "part", [P, 1])
                before = sb(ctx, "before", [P, GROUPS])
                cnt = sb(ctx, "cnt", [P, 1])
                pos = sb(ctx, "pos", [P, 1])
                step = sb(ctx, "step", [P, TS])
                passed = sb(ctx, "passed", [P, TS])
                grp = sb(ctx, "grp", [1, TS])
                grp_c = sb(ctx, "grp_c", [1, TS])
                neg = sb(ctx, "neg", [1, TS])
                win = sb(ctx, "win", [1, TS])
                grp_col = sb(ctx, "grp_col", [P, TCH], I32)
                win_col = sb(ctx, "win_col", [P, TCH])
                eidx = sb(ctx, "eidx", [P, 2, TCH, GE], I32)
                rel = sb(ctx, "rel", [P, TCH, GE])
                inw = sb(ctx, "inw", [P, TCH, GE])
                off = sb(ctx, "off", [P, TCH, GE])
                idf = sb(ctx, "idf", [P, TCH, GE])
                ps_f = pb(ctx, "ps_f", [P, 512])
                ps_b = pb(ctx, "ps_b", [P, 512])
                ps_c = pb(ctx, "ps_c", [P, 512])
                ps_t = [pb(ctx, f"ps_t{k}", [P, 512]) for k in range(2)]

                filled, padded, got_first = sem("filled"), sem("padded"), sem("got_first")
                made, const = sem("made"), sem("const")
                first_f, first_b, counted = sem("first_f"), sem("first_b"), sem("counted")
                summed_b, table_row, cols_ps, cols_sb = sem("summed_b"), sem("table_row"), sem("cols_ps"), sem("cols_sb")
                rows_got, masked, turned, stored = sem("rows_got"), sem("masked"), sem("turned"), sem("stored")
                chain = sem("chain")

                @nc_block()
                def _(block):
                    @block.sync
                    def _(sp):
                        sp.dma_start(first_i[:, :], dst[:].rearrange("(a e) -> a e", a=1)[:, 0:E:GE],
                                     allow_slow_non_contiguous=True).then_inc(got_first, 16)
                        for pad, given in ((src_pad, src), (dst_pad, dst)):
                            flat = pad.rearrange("a b -> (a b)")
                            sp.dma_start(flat[0:E].rearrange("(a b) -> a b", a=16),
                                         given[:].rearrange("(a b) -> a b", a=16)).then_inc(padded, 16)
                        sp.wait_ge(filled, 2)
                        for k, pad in enumerate((src_pad, dst_pad)):
                            flat = pad.rearrange("a b -> (a b)")
                            sp.dma_start(flat[E:E + TAIL].rearrange("(a b) -> a b", a=1),
                                         fill[:, k, :]).then_inc(padded, 16)

                    @block.gpsimd
                    def _(pool):
                        nc.gpsimd.memset(fill[:, 0, :], 0).then_inc(filled, 1)
                        nc.gpsimd.memset(fill[:, 1, :], WINDOWS * P).then_inc(filled, 1)
                        nc.gpsimd.memset(ident[:, :], 0.0).then_inc(made, 1)
                        nc.gpsimd.memset(ones[:, :], 1.0).then_inc(const, 1)
                        exact = dict(allow_small_or_imprecise_dtypes=True)
                        nc.gpsimd.iota(bound[:, :], pattern=[[0, 1]], base=P, channel_multiplier=P, **exact).then_inc(const, 1)
                        nc.gpsimd.iota(part[:, :], pattern=[[0, 1]], base=0, channel_multiplier=1, **exact).then_inc(const, 1)
                        nc.gpsimd.iota(step[:, :], pattern=[[1, TS]], base=0, channel_multiplier=0, **exact).then_inc(const, 1)
                        nc.gpsimd.iota(lane[:, :], pattern=[[1, P]], base=0, channel_multiplier=0, **exact).then_inc(const, 1)
                        pool.wait_ge(made, 1)
                        nc.gpsimd.affine_select(out=ident[:, :], in_=ident[:, :], compare_op=ALU.not_equal, fill=1.0,
                                                base=0, pattern=[[-1, P]], channel_multiplier=1).then_inc(const, 1)
                        pool.wait_ge(padded, 64)
                        pool.wait_ge(cols_sb, 1)
                        for c in range(TCH):
                            for k, pad in enumerate((src_pad, dst_pad)):
                                pool.indirect_dma_start(
                                    eidx[:, k, c, :], None, pad[:, :],
                                    bass.IndirectOffsetOnAxis(grp_col[:, c:c + 1], 0)).then_inc(rows_got, 16)

                    @block.tensor
                    def _(pe):
                        pe.wait_ge(const, 6)
                        pe.wait_ge(first_f, 1)
                        nc.tensor.matmul(ps_f[:, 0:GROUPS], ones[0:1, :], first[0:1, :], start=True, stop=True).then_inc(first_b, 1)
                        pe.wait_ge(counted, 1)
                        nc.tensor.matmul(ps_b[:, 0:TS], ones[0:WINDOWS - 1, :], passed[0:WINDOWS - 1, :],
                                         start=True, stop=True).then_inc(summed_b, 1)
                        pe.wait_ge(table_row, 1)
                        for k, row in enumerate((grp_c, win)):
                            for c in range(TCH):
                                last = nc.tensor.matmul(ps_c[:, 2 * (k * TCH + c):2 * (k * TCH + c) + 1],
                                                        row[0:1, c * P:(c + 1) * P], ones[0:1, 0:1], start=True, stop=True)
                        last.then_inc(cols_ps, 1)
                        for n, (table, c) in enumerate((t, c) for t in range(2) for c in range(TCH)):
                            if n < TCH:
                                pe.wait_ge(masked, c + 1)
                            if n >= 2:
                                pe.wait_ge(stored, n - 1)
                            given = (rel, idf)[table][:, c, :]
                            for g in range(G):
                                last = nc.tensor.transpose(ps_t[n % 2][:, g * P:(g + 1) * P],
                                                           given[:, g * P:(g + 1) * P], ident[:, :])
                            last.then_inc(turned, 1)

                    @block.vector
                    def _(dve):
                        done = [0]

                        def then(ins):
                            done[0] += 1
                            ins.then_inc(chain, 1)
                            dve.wait_ge(chain, done[0])

                        dve.wait_ge(const, 6)
                        dve.wait_ge(got_first, 16)
                        nc.vector.tensor_copy(first[:, :], first_i[:, :]).then_inc(first_f, 1)
                        dve.wait_ge(first_b, 1)
                        then(nc.vector.tensor_scalar(before[:, :], ps_f[:, 0:GROUPS], bound[:, 0:1], None, ALU.is_lt))
                        then(nc.vector.tensor_reduce(cnt[:, :], before[:, :], AX, ALU.add))
                        then(nc.vector.tensor_tensor(pos[:, :], cnt[:, :], part[:, :], ALU.add))
                        nc.vector.tensor_scalar(passed[:, :], step[:, :], pos[:, 0:1], None, ALU.is_ge).then_inc(counted, 1)
                        dve.wait_ge(summed_b, 1)
                        then(nc.vector.tensor_tensor(grp[:, :], step[0:1, :], ps_b[0:1, 0:TS], ALU.subtract))
                        then(nc.vector.tensor_scalar(neg[:, :], grp[:, :], 0.0, None, ALU.is_lt))
                        then(nc.vector.tensor_tensor(win[:, :], ps_b[0:1, 0:TS], neg[:, :], ALU.subtract))
                        then(nc.vector.tensor_scalar(col_t[:, :], win[:, :], float(WIDTH), None, ALU.mult))
                        nc.vector.tensor_scalar(grp_c[:, :], grp[:, :], 0.0, float(GROUPS), ALU.max, ALU.min).then_inc(table_row, 1)
                        then(nc.vector.tensor_scalar(row_t[:, :], win[:, :], float(P), None, ALU.mult))
                        then(nc.vector.tensor_copy(qcol_t[:, :], win[:, :]))
                        then(nc.vector.tensor_scalar(par_t[:, :], qcol_t[:, :], 1, None, ALU.bitwise_and))
                        then(nc.vector.tensor_scalar(par_t[:, :], par_t[:, :], float(D), None, ALU.mult))
                        then(nc.vector.memset(zero[:, :].bitcast(F32), 0.0))
                        then(nc.vector.tensor_scalar(qcol_t[:, :], qcol_t[:, :], QB - 1, None, ALU.bitwise_and))
                        then(nc.vector.tensor_scalar(qcol_t[:, :], qcol_t[:, :], float(2 * D), None, ALU.mult))
                        then(nc.vector.memset(new_t[:, 0:1], 1))
                        then(nc.vector.tensor_tensor(new_t[:, 1:TS], win[:, 1:TS], win[:, 0:TS - 1], ALU.not_equal))
                        dve.wait_ge(cols_ps, 1)
                        then(nc.vector.tensor_copy(grp_col[:, :], ps_c[:, 0:2 * TCH:2]))
                        then(nc.vector.tensor_scalar(win_col[:, :], ps_c[:, 2 * TCH:4 * TCH:2], float(P), None, ALU.mult))
                        dve.sem_inc(cols_sb, 1)

                        dve.wait_ge(rows_got, 16 * 2 * TCH)
                        for c in range(TCH):
                            then(nc.vector.tensor_scalar(rel[:, c, :], eidx[:, 1, c, :], win_col[:, c:c + 1], None, ALU.subtract))
                            then(nc.vector.tensor_scalar(inw[:, c, :], rel[:, c, :], 0.0, None, ALU.is_ge))
                            then(nc.vector.scalar_tensor_tensor(off[:, c, :], rel[:, c, :], float(P), inw[:, c, :],
                                                                ALU.is_lt, ALU.mult))
                            then(nc.vector.tensor_scalar(inw[:, c, :], off[:, c, :], -float(OUTSIDE), float(OUTSIDE),
                                                         ALU.mult, ALU.add))
                            nc.vector.tensor_tensor(idf[:, c, :], eidx[:, 0, c, :], inw[:, c, :], ALU.add).then_inc(masked, 1)
                        for n, (table, c) in enumerate((t, c) for t in range(2) for c in range(TCH)):
                            dve.wait_ge(turned, n + 1)
                            to = (rel_t, src_t)[table][:, c * P * G:(c + 1) * P * G]
                            nc.vector.tensor_copy(to.rearrange("p (s g) -> p g s", g=G),
                                                  ps_t[n % 2][:, 0:GE].rearrange("p (g s) -> p g s", g=G)).then_inc(stored, 1)

        def dense(layer, given, A_bc=None, C_bc=None):
            M = len(given)
            tag = str(layer)
            with ExitStack() as ctx:
                w_hi = sb(ctx, "w_hi" + tag, [P, M, KC, D], F32R)
                w_lo = sb(ctx, "w_lo" + tag, [P, M, KC, D], F32R)
                x_sb = sb(ctx, "x_sb" + tag, [P, 2, D])
                x1 = sb(ctx, "x1_sb", [P, 2, D]) if layer else x_sb
                h = sb(ctx, "h" + tag, [P, 2, D])
                st = sb(ctx, "st" + tag, [P, 6])
                mv = sb(ctx, "mv" + tag, [P, 2])
                sd = sb(ctx, "sd" + tag, [P, 1])
                rs = sb(ctx, "rs" + tag, [P, 2])
                nb = sb(ctx, "nb" + tag, [P, 2])
                hT_hi = sb(ctx, "hT_hi" + tag, [P, 2, D], F32R)
                hT_lo = sb(ctx, "hT_lo" + tag, [P, 2, D], F32R)
                o_sb = sb(ctx, "o_sb" + tag, [P, 2, 2, D])
                w_st = [o_sb[:, :, :, :].rearrange("p a b d -> p (a b) d")]
                if layer:
                    q_sb = sb(ctx, "q_sb", [P, 2, 2, D], F32R)
                    w_st.append(q_sb[:, :, :, :].rearrange("p a b d -> p (a b) d").bitcast(F32))
                else:
                    b_row = sb(ctx, "b_row", [1, D])
                    b_bc = sb(ctx, "b_bc", [P, D])
                ps_t = [pb(ctx, f"ps_t{tag}{k}", [P, 512]) for k in range(2)]
                ps_o = [[pb(ctx, f"ps_o{tag}{k}{j}", [P, 512]) for j in range(M)] for k in range(2)]

                w_in, w_turned, w_high, w_split, b_in = sems("w_in" + tag, M), *(
                    sem(n + tag) for n in ("w_turned", "w_high", "w_split", "b_in"))
                x_in, t_made, t_sum, normal = sems("x_in" + tag, 2), sem("t_made" + tag), sem("t_sum" + tag), sem("normal" + tag)
                var_ready, dev_ready, shift_ready, h_made = (sem(n + tag) for n in ("var_ready", "dev_ready", "shift_ready", "h_made"))
                q_high = sem("q_high" + tag)
                turned, high, split, made, by_act, by_dve = (
                    sem(n + tag) for n in ("turned", "high", "split", "made", "by_act", "by_dve"))
                kept, stored = sems("kept" + tag, 2), sems("stored" + tag, 2)

                def later(w):
                    return not isinstance(w, int) or w >= 2

                @nc_block()
                def _(block):
                    @block.sync
                    def _(sp):
                        def load(w, par, n=P):
                            if later(w):
                                sp.wait_ge(t_made if layer else h_made, w - 1)
                            sp.dma_start(x_sb[0:n, par, :], x[ds(w * P, n), :]).then_inc(x_in[par], 16)

                        def keep(w, par):
                            sp.wait_ge(h_made, w + 1)
                            sp.dma_start(x1_d[ds(w * P, P), :], x1[:, par, :]).then_inc(kept[par], 16)
                            sp.dma_start(h1_d[ds(w * P, P), :], h[:, par, :]).then_inc(kept[par], 16)

                        def store(w, par):
                            sp.wait_ge(by_act, w + 1)
                            sp.wait_ge(by_dve, w + 1)
                            rows = ds(w * P, P)
                            if layer:
                                sp.dma_start(q_d[rows, :], q_sb[:, par, :, :].rearrange("p a d -> p (a d)").bitcast(F32)).then_inc(stored[par], 16)
                                sp.dma_start(kv_d[rows, :], o_sb[:, par, :, :].rearrange("p a d -> p (a d)")).then_inc(stored[par], 16)
                            else:
                                sp.dma_start(y_d[rows, :], o_sb[:, par, 0, :]).then_inc(stored[par], 16)
                                sp.dma_start(z_d[rows, :], o_sb[:, par, 1, :]).then_inc(stored[par], 16)

                        def both(w, par, n=P):
                            load(w + 3, 1 - par, n)
                            if layer:
                                keep(w + 1, 1 - par)
                            store(w, par)

                        load(0, 0)
                        load(1, 1)
                        if not layer:
                            sp.dma_start(b_row[:, :], b_l[:].rearrange("(a n) -> a n", a=1)).then_inc(b_in, 16)
                        for k, w in enumerate(given):
                            if k >= len(w_st):
                                sp.wait_ge(w_split, (k - len(w_st) + 1) * KC)
                            sp.dma_start(w_st[k % len(w_st)], w[:, :].rearrange("(c p) i -> p c i", p=P)).then_inc(w_in[k], 16)
                        load(2, 0)
                        if layer:
                            keep(0, 0)
                        both(0, 0)
                        with sp.Fori(0, PAIRS - 2) as i:
                            for par in range(2):
                                both(2 * i + par + 1, 1 - par)
                        both(WINDOWS - 4, 1, LAST)
                        for w in range(WINDOWS - 3, WINDOWS):
                            if layer and w < WINDOWS - 1:
                                keep(w + 1, 1 - w % 2)
                            store(w, w % 2)
                        for par in range(2):
                            if layer:
                                sp.wait_ge(kept[par], 32 * (PAIRS + 1 - par))
                            sp.wait_ge(stored[par], 32 * (PAIRS + 1 - par))

                    if layer:
                        @block.gpsimd
                        def _(pool):
                            def shift(w, i, par):
                                pool.wait_ge(x_in[par], 16 * (i + 1))
                                nc.gpsimd.tensor_tensor(x_sb[:, par, :], x_sb[:, par, :], C_bc[:, :], ALU.add).then_inc(t_sum, 1)

                            with pool.Fori(0, PAIRS) as i:
                                for par in range(2):
                                    shift(2 * i + par, i, par)
                            shift(WINDOWS - 1, PAIRS, 0)

                    @block.vector
                    def _(dve):
                        def part_low(n, source, lo, hi, of, count):
                            dve.wait_ge(of, n + 1)
                            nc.vector.tensor_tensor(lo, source, hi.bitcast(F32), ALU.subtract).then_inc(count, 1)

                        for k in range(M):
                            for c in range(KC):
                                n = k * KC + c
                                part_low(n, w_st[k % 2][:, c, :] if layer else ps_o[n % 2][0][:, :],
                                         w_lo[:, k, c, :], w_hi[:, k, c, :], w_high, w_split)
                        if not layer:
                            dve.wait_ge(w_turned, M * KC + 1)
                            nc.vector.tensor_copy(b_bc[:, :], ps_o[0][1][:, :]).then_inc(w_split, 1)
                            dve.wait_ge(w_split, M * KC + 1)

                        def statistics(w, i, par):
                            at = w * 6

                            def then(ins, k):
                                ins.then_inc(normal, 1)
                                dve.wait_ge(normal, at + k)

                            if layer:
                                if later(w):
                                    dve.wait_ge(kept[par], 32 * i)
                                then(nc.vector.tensor_tensor(x1[:, par, :], window(w), A_bc[:, :], ALU.mult), 1)
                                dve.wait_ge(t_sum, w + 1)
                                then(nc.vector.tensor_tensor(x1[:, par, :], x1[:, par, :], x_sb[:, par, :], ALU.add), 2)
                                dve.sem_inc(t_made, 1)
                            else:
                                dve.wait_ge(x_in[par], 16 * (i + 1))
                                dve.sem_inc(normal, 2)
                            then(nc.vector.bn_stats(st[:, :], x1[:, par, :]), 3)
                            alone(dve)
                            then(nc.vector.bn_aggr(mv[:, :], st[:, :]), 4)
                            nc.vector.tensor_scalar(sd[:, :], mv[:, 1:2], EPS, None, ALU.add).then_inc(var_ready, 1)
                            dve.wait_ge(dev_ready, w + 1)
                            if later(w):
                                dve.wait_ge(h_made, w - 1)
                            then(nc.vector.reciprocal(rs[:, par:par + 1], sd[:, :]), 5)
                            then(nc.vector.scalar_tensor_tensor(nb[:, par:par + 1], mv[:, 0:1], -1.0, rs[:, par:par + 1],
                                                                ALU.mult, ALU.mult), 6)
                            dve.sem_inc(shift_ready, 1)

                        def split_h(w, par):
                            if later(w):
                                dve.wait_ge(made, M * (w - 1))
                            part_low(w, ps_t[par][:, :], hT_lo[:, par, :], hT_hi[:, par, :], high, split)

                        def read(w, i, par):
                            dve.wait_ge(made, M * w + 2)
                            if later(w):
                                dve.wait_ge(stored[par], 32 * i)
                            if layer:
                                nc.vector.tensor_copy(o_sb[:, par, 0, :], ps_o[par][1][:, :])
                                dve.wait_ge(q_high, w + 1)
                                nc.vector.scalar_tensor_tensor(q_sb[:, par, 1, :], ps_o[par][0][:, :], DH ** -0.5,
                                                               q_sb[:, par, 0, :].bitcast(F32), ALU.mult, ALU.subtract).then_inc(by_dve, 1)
                            else:
                                nc.vector.tensor_tensor(o_sb[:, par, 1, :], ps_o[par][1][:, :], b_bc[:, :], ALU.add).then_inc(by_dve, 1)

                        statistics(0, 0, 0)
                        statistics(1, 0, 1)
                        split_h(0, 0)
                        for w in range(2):
                            split_h(w + 1, 1 - w)
                            statistics(w + 2, 1, w)
                            read(w, 0, w)
                        with dve.Fori(1, PAIRS - 1) as i:
                            for par in range(2):
                                split_h(2 * i + par + 1, 1 - par)
                                statistics(2 * i + par + 2, i + 1, par)
                                read(2 * i + par, i, par)
                        for w in range(WINDOWS - 3, WINDOWS):
                            if w < WINDOWS - 1:
                                split_h(w + 1, 1 - w % 2)
                            if w < WINDOWS - 2:
                                statistics(w + 2, w // 2 + 1, w % 2)
                            read(w, w // 2, w % 2)

                    @block.scalar
                    def _(act):
                        for k in range(M):
                            for c in range(KC):
                                n = k * KC + c
                                if layer:
                                    act.wait_ge(w_in[k], 16)
                                else:
                                    act.wait_ge(w_turned, n + 1)
                                nc.scalar.copy(w_hi[:, k, c, :], w_st[k % 2][:, c, :] if layer else ps_o[n % 2][0][:, :]).then_inc(w_high, 1)

                        def norm(w, i, par):
                            act.wait_ge(var_ready, w + 1)
                            nc.scalar.activation(sd[:, :], sd[:, :], ACT.Sqrt).then_inc(dev_ready, 1)
                            act.wait_ge(shift_ready, w + 1)
                            if later(w):
                                if layer:
                                    act.wait_ge(kept[par], 32 * i)
                                act.wait_ge(turned, w - 1)
                            nc.scalar.activation(h[:, par, :], x1[:, par, :], ACT.Relu, bias=nb[:, par:par + 1],
                                                 scale=rs[:, par:par + 1]).then_inc(h_made, 1)

                        def high_h(w, par):
                            act.wait_ge(turned, w + 1)
                            if later(w):
                                act.wait_ge(made, M * (w - 1))
                            nc.scalar.copy(hT_hi[:, par, :], ps_t[par][:, :]).then_inc(high, 1)

                        def read(w, i, par):
                            act.wait_ge(made, M * w + M if layer else M * w + 1)
                            if later(w):
                                act.wait_ge(stored[par], 32 * i)
                            if layer:
                                nc.scalar.activation(q_sb[:, par, 0, :], ps_o[par][0][:, :], ACT.Copy, scale=DH ** -0.5).then_inc(q_high, 1)
                                nc.scalar.copy(o_sb[:, par, 1, :], ps_o[par][2][:, :]).then_inc(by_act, 1)
                            else:
                                nc.scalar.copy(o_sb[:, par, 0, :], ps_o[par][0][:, :]).then_inc(by_act, 1)

                        norm(0, 0, 0)
                        norm(1, 0, 1)
                        high_h(0, 0)
                        for w in range(2):
                            high_h(w + 1, 1 - w)
                            norm(w + 2, 1, w)
                            read(w, 0, w)
                        with act.Fori(1, PAIRS - 1) as i:
                            for par in range(2):
                                high_h(2 * i + par + 1, 1 - par)
                                norm(2 * i + par + 2, i + 1, par)
                                read(2 * i + par, i, par)
                        for w in range(WINDOWS - 3, WINDOWS):
                            if w < WINDOWS - 1:
                                high_h(w + 1, 1 - w % 2)
                            if w < WINDOWS - 2:
                                norm(w + 2, w // 2 + 1, w % 2)
                            read(w, w // 2, w % 2)

                    @block.tensor
                    def _(pe):
                        if not layer:
                            for k in range(M):
                                pe.wait_ge(w_in[k], 16)
                                for c in range(KC):
                                    n = k * KC + c
                                    if n >= 2:
                                        pe.wait_ge(w_split, n - 1)
                                    for o in range(KC):
                                        last = nc.tensor.transpose(ps_o[n % 2][0][:, o * P:(o + 1) * P],
                                                                   w_st[0][:, o, c * P:(c + 1) * P], ident[:, :])
                                    last.then_inc(w_turned, 1)
                            pe.wait_ge(b_in, 16)
                            nc.tensor.matmul(ps_o[0][1][:, :], ones[0:1, :], b_row[0:1, :], start=True, stop=True).then_inc(w_turned, 1)

                        def turn(w, par):
                            pe.wait_ge(h_made, w + 1)
                            if later(w):
                                pe.wait_ge(split, w - 1)
                            for c in range(KC):
                                last = nc.tensor.transpose(ps_t[par][:, c * P:(c + 1) * P], h[:, par, c * P:(c + 1) * P], ident[:, :])
                            last.then_inc(turned, 1)

                        def products(w, par):
                            pe.wait_ge(split, w + 1)
                            if later(w):
                                pe.wait_ge(by_dve, w - 1)
                                pe.wait_ge(by_act, w - 1)
                            for k in range(M):
                                for c in range(KC):
                                    hi, lo = (t[:, par, c * P:(c + 1) * P] for t in (hT_hi, hT_lo))
                                    for j, (a, b) in enumerate(((hi, w_hi), (hi, w_lo), (lo, w_hi))):
                                        last = nc.tensor.matmul(ps_o[par][k][:, :], a, b[:, k, c, :],
                                                                start=(c == 0 and j == 0), stop=(c == KC - 1 and j == 2))
                                last.then_inc(made, 1)

                        turn(0, 0)
                        pe.wait_ge(w_split, M * KC + (0 if layer else 1))
                        for w in range(2):
                            turn(w + 1, 1 - w)
                            products(w, w)
                        with pe.Fori(1, PAIRS) as i:
                            for par in range(2):
                                turn(2 * i + par + 1, 1 - par)
                                products(2 * i + par, par)
                        products(WINDOWS - 1, 0)

        def aggregate():
            with ExitStack() as ctx:
                rows = sb(ctx, "rows", [P, U, G, D])
                hot = sb(ctx, "hot", [P, U, G, P], F32R)
                ones_r = sb(ctx, "ones_r", [P, 2], F32R)
                spare = sb(ctx, "spare", [1, 2])
                idx = sb(ctx, "idx", [P, U // H, H * G], I32)
                pss = pb(ctx, "pss", [P, 2 * D])
                psc = pb(ctx, "psc", [P, 512])
                cleared, staged, rows_in = sem("cleared"), sem("staged"), sems("rows_in", U)
                hot_made, ps_made = sem("hot_made"), sem("ps_made")

                @nc_block()
                def _(block):
                    @block.scalar
                    def _(act):
                        def stage(i, part):
                            nc.scalar.copy(idx[:, part, :], src_t[:, ds((i * U + part * H) * G, H * G)]).then_inc(staged, 1)

                        for part in range(U // H):
                            stage(0, part)
                        with act.Fori(0, ITERS) as i:
                            for part in range(U // H):
                                for u in range(part * H, part * H + H):
                                    act.wait_ge(rows_in[u], (i + 1) * 16 * G)
                                alone(act)
                                stage(i + 1, part)

                    @block.gpsimd
                    def _(pool):
                        limit = pool.alloc_register("limit0")
                        pool.reg_mov(limit, N - 1)

                        def gather(i, u):
                            if u % H == 0:
                                if isinstance(i, int):
                                    pool.wait_ge(cleared, u + H)
                                pool.wait_ge(staged, i * (U // H) + u // H + 1)
                                pool.wait_ge(ps_made, i * U + u + H)
                                alone(pool)
                            for g in range(G):
                                k = (u % H) * G + g
                                pool.indirect_dma_start(rows[:, u, g, :], None, y_d[0:N, :],
                                                        bass.IndirectOffsetOnAxis(idx[:, u // H, k:k + 1], 0),
                                                        bounds_check=limit, oob_is_err=False).then_inc(rows_in[u], 16)

                        for u in range(U):
                            gather(0, u)
                        with pool.Fori(1, ITERS) as i:
                            for u in range(U):
                                gather(i, u)

                    @block.vector
                    def _(dve):
                        nc.vector.tensor_copy(ones_r[:, :], ones[:, 0:2])
                        for u in range(U):
                            nc.vector.memset(rows[:, u, :, :], 0.0).then_inc(cleared, 1)

                        def one_hot(i, u):
                            s = i * U + u
                            dve.wait_ge(ps_made, s + 1)
                            nc.vector.tensor_tensor(hot[:, u, :, :], lane[:, :].unsqueeze(1).to_broadcast([P, G, P]),
                                                    rel_t[:, ds(s * G, G)].unsqueeze(2).to_broadcast([P, G, P]),
                                                    ALU.is_equal).then_inc(hot_made, 1)

                        def flush(s):
                            [new] = load_values(mybir.EngineType.DVE, new_t, s, 1, 1)
                            flush_before(dve, pss, psc, 1, s, new, ps_made, U)

                        for u in range(U):
                            one_hot(0, u)
                            if u >= 2:
                                flush(u - 1)
                        with dve.Fori(1, ITERS) as i:
                            for u in range(U):
                                one_hot(i, u)
                                flush(i * U + u - 1)
                        nc.vector.memset(spare[:, 0:1], 0.0).then_inc(hot_made, 1)
                        flush(STEPS - 1)
                        nc.vector.memset(spare[:, 1:2], 0.0).then_inc(hot_made, 1)
                        dve.wait_ge(ps_made, U + STEPS)
                        flush_last(pss, psc, 1)

                    @block.tensor
                    def _(pe):
                        pe.sem_inc(ps_made, U)
                        with pe.Fori(0, ITERS) as i:
                            for u in range(U):
                                s = i * U + u
                                [par] = load_values(mybir.EngineType.PE, par_t, s, 1, D)
                                [new] = load_values(mybir.EngineType.PE, new_t, s, 1, 1)
                                pe.wait_ge(hot_made, s + 2)
                                open_window(pe, pss, par, new)
                                pe.wait_ge(rows_in[u], (i + 1) * 16 * G)
                                for g in range(G):
                                    nc.tensor.matmul(pss[:, ds(par, D)], hot[:, u, g, :].bitcast(F32), rows[:, u, g, :],
                                                     start=False, stop=(g == G - 1), skip_group_check=True)
                                pe.wait_ge(hot_made, s + 3)
                                open_counts(pe, psc, new)
                                for g in range(G):
                                    last = nc.tensor.matmul(psc[:, 0:2], hot[:, u, g, :], ones_r[:, :],
                                                            start=False, stop=(g == G - 1), skip_group_check=True)
                                last.then_inc(ps_made, 1)

        def load_values(engine, table, s, n, most):
            _, values = nc.values_load_multi_w_load_instructions(
                table[0:1, ds(s, n)], engines=[engine], min_val=0, max_val=most,
                skip_runtime_bounds_check_because="a step's window is one of 0..WINDOWS-1 by how the tables are made")
            return values

        def open_window(pe, pss, par, new):
            with pe.If(new):
                nc.tensor.matmul(pss[:, ds(par, D)], zero[0:1, 0:P], zero[0:1, :], start=True, stop=False, skip_group_check=True)

        def open_counts(pe, psc, new):
            with pe.If(new):
                nc.tensor.matmul(psc[:, 0:2 * HEADS], zero[0:1, 0:P], zero[0:1, 0:2 * HEADS], start=True, stop=False, skip_group_check=True)

        def copy_counts(col, psc, width):
            to = sums[:, ds(col + D, width)]
            if width == 1:
                nc.vector.tensor_copy(to, psc[:, 0:1])
            else:
                nc.vector.tensor_reduce(to, psc[:, 0:2 * width].rearrange("p (t h) -> p h t", t=2), AX, ALU.add)

        def flush_before(dve, pss, psc, width, s, new, ps_made, lead):
            with dve.If(new):
                [col] = load_values(mybir.EngineType.DVE, col_t, s - 1, 1, (WINDOWS - 1) * WIDTH)
                [par] = load_values(mybir.EngineType.DVE, par_t, s - 1, 1, D)
                dve.wait_ge(ps_made, s + lead)
                alone(dve)
                copy_counts(col, psc, width)
                nc.vector.tensor_copy(sums[:, ds(col, D)], pss[:, ds(par, D)])

        def flush_last(pss, psc, width):
            par = (WINDOWS - 1) % 2 * D
            nc.vector.tensor_copy(window(WINDOWS - 1), pss[:, par:par + D])
            copy_counts((WINDOWS - 1) * WIDTH, psc, width)

        def column_sums(pe, ps, ready, lead, summed):
            def total(w, n=P):
                pe.wait_ge(ready, w + lead + 1)
                nc.tensor.matmul(ps[:, :], ones[0:n, :], window(w)[0:n, :], start=isinstance(w, int) and w == 0,
                                 stop=isinstance(w, int) and w == WINDOWS - 1).then_inc(summed, 1)

            for w in range(NB):
                total(w)
            with pe.Fori(1, FOURS) as i:
                for b in range(NB):
                    total(NB * i + b)
            total(WINDOWS - 1, LAST)

        def share_of(S1, ps):
            nc.vector.tensor_scalar(S1[:, :], ps[:, :], 1.0 / P, None, ALU.mult)

        def combine(S1, S2):
            with ExitStack() as ctx:
                z = sb(ctx, "z_sb", [P, NB, D])
                rd = sb(ctx, "rd", [P, WINDOWS])
                sq = sb(ctx, "sq", [P, NB, D])
                S2_odd = sb(ctx, "S2_odd", [P, D])
                ps_1 = pb(ctx, "ps_1a", [P, 512])
                z_in, degrees, added_z, rect, squared, zero2, summed1, summed2, zero3, summed3 = (
                    sems("z_in", NB), sem("degrees"), sem("added_z"), sem("rect"), sem("squared"), sem("zero2"),
                    sem("summed1"), sem("summed2"), sem("zero3"), sem("summed3"))

                @nc_block()
                def _(block):
                    @block.sync
                    def _(sp):
                        def load(w, par):
                            sp.wait_ge(added_z, w + 1)
                            sp.dma_start(z[:, par, :], z_d[ds(w * P, P), :]).then_inc(z_in[par], 16)

                        with sp.Fori(0, FOURS) as i:
                            for par in range(NB):
                                load(NB * i + par, par)
                        load(WINDOWS - 1, 0)

                    @block.vector
                    def _(dve):
                        degree = sums[:, :].rearrange("p (w c) -> p w c", c=WIDTH)[:, :, D]
                        nc.vector.tensor_scalar(rd[:, :], degree, 1.0, None, ALU.max).then_inc(degrees, 1)
                        dve.wait_ge(degrees, 1)
                        nc.vector.reciprocal(rd[:, :], rd[:, :]).then_inc(degrees, 1)
                        dve.wait_ge(degrees, 2)
                        spread = sums[:, :].rearrange("p (w c) -> p w c", c=WIDTH)[:, :, D + 1]
                        nc.vector.tensor_copy(spread, rd[:, :]).then_inc(degrees, 1)
                        dve.wait_ge(degrees, 3)
                        dve.sem_inc(added_z, NB)

                        def add_z(w, i, par):
                            dve.wait_ge(z_in[par], 16 * (i + 1))
                            alone(dve)
                            nc.vector.scalar_tensor_tensor(window(w), window(w), sums[:, ds(w * WIDTH + D + 1, 1)], z[:, par, :],
                                                           ALU.mult, ALU.add).then_inc(added_z, 1)

                        nc.vector.memset(S2_odd[:, :], 0.0).then_inc(zero3, 1)
                        dve.wait_ge(zero3, 1)

                        def add_square(i, par):
                            dve.wait_ge(squared, NB * i + par + 1)
                            nc.vector.tensor_tensor(S2_odd[:, :], S2_odd[:, :], sq[:, par, :], ALU.add).then_inc(summed3, 1)
                            dve.wait_ge(summed3, NB // 2 * i + par // 2 + 1)

                        for par in range(NB):
                            add_z(par, 0, par)
                        with dve.Fori(0, FOURS - 1) as i:
                            for par in range(NB):
                                add_z(NB * i + par + NB, i + 1, par)
                                if par % 2:
                                    add_square(i, par)
                        add_z(WINDOWS - 1, FOURS, 0)
                        for par in range(1, NB, 2):
                            add_square(FOURS - 1, par)
                        dve.wait_ge(summed2, NB // 2 * FOURS + 1)
                        nc.vector.tensor_tensor(S2[:, :], S2[:, :], S2_odd[:, :], ALU.add)
                        dve.wait_ge(summed1, WINDOWS)
                        share_of(S1, ps_1)

                    @block.tensor
                    def _(pe):
                        column_sums(pe, ps_1, rect, 0, summed1)

                    @block.scalar
                    def _(act):
                        def rectify(w):
                            act.wait_ge(added_z, w + NB + 1)
                            alone(act)
                            nc.scalar.activation(window(w), window(w), ACT.Relu).then_inc(rect, 1)

                        def square(w, i, par):
                            act.wait_ge(rect, w + 1)
                            if not isinstance(i, int) or i:
                                act.wait_ge((summed2, summed3)[par % 2], NB // 2 * (i - 1) + par // 2 + 1)
                            alone(act)
                            nc.scalar.activation(sq[:, par, :], window(w), ACT.Square).then_inc(squared, 1)

                        rectify(0)
                        for w in range(NB):
                            rectify(w + 1)
                            square(w, 0, w)
                        with act.Fori(1, FOURS) as i:
                            for par in range(NB):
                                rectify(NB * i + par + 1)
                                square(NB * i + par, i, par)
                        square(WINDOWS - 1, FOURS, 0)

                    @block.gpsimd
                    def _(pool):
                        nc.gpsimd.memset(S2[:, :], 0.0).then_inc(zero2, 1)
                        pool.wait_ge(zero2, 1)

                        def add_square(i, par, n=P):
                            pool.wait_ge(squared, NB * i + par + 1)
                            nc.gpsimd.tensor_tensor(S2[0:n, :], S2[0:n, :], sq[0:n, par, :], ALU.add).then_inc(summed2, 1)
                            pool.wait_ge(summed2, NB // 2 * i + par // 2 + 1)

                        with pool.Fori(0, FOURS) as i:
                            for par in range(0, NB, 2):
                                add_square(i, par)
                        add_square(FOURS, 0, LAST)

        def batch_norm(tag, before, gamma, beta, after):
            with ExitStack() as ctx:
                A_bc = sb(ctx, "A_bc" + tag, [P, D])
                C_bc = sb(ctx, "C_bc" + tag, [P, D])
                with ExitStack() as inner:
                    S1 = sb(inner, "S1" + tag, [P, D])
                    S2 = sb(inner, "S2" + tag, [P, D])
                    before(S1, S2)
                    coefficients(tag, gamma, beta, S1, S2, A_bc, C_bc)
                after(A_bc, C_bc)

        def coefficients(tag, gamma, beta, S1, S2, A_bc, C_bc):
            with ExitStack() as ctx:
                gb = sb(ctx, "gb" + tag, [1, 2, D])
                mu = sb(ctx, "mu" + tag, [P, D])
                var = sb(ctx, "var" + tag, [P, D])
                ps_s = [pb(ctx, f"ps_s{tag}{k}", [P, 512]) for k in range(4)]
                gb_in, tot, chain, var_ready, dev_ready = (sem(n + tag) for n in ("gb_in", "tot", "cchain", "bn_var", "bn_dev"))

                @nc_block()
                def _(block):
                    @block.sync
                    def _(sp):
                        for k, v in enumerate((gamma, beta)):
                            sp.dma_start(gb[:, k, :], v[:].rearrange("(a n) -> a n", a=1)).then_inc(gb_in, 16)

                    @block.tensor
                    def _(pe):
                        nc.tensor.matmul(ps_s[0][:, :], ones[:, :], S1[:, :], start=True, stop=True).then_inc(tot, 1)
                        nc.tensor.matmul(ps_s[1][:, :], ones[:, :], S2[:, :], start=True, stop=True).then_inc(tot, 1)
                        pe.wait_ge(gb_in, 32)
                        for k in range(2):
                            nc.tensor.matmul(ps_s[2 + k][:, :], ones[0:1, :], gb[0:1, k, :], start=True, stop=True).then_inc(tot, 1)

                    @block.vector
                    def _(dve):
                        done = [0]

                        def then(ins):
                            done[0] += 1
                            ins.then_inc(chain, 1)
                            dve.wait_ge(chain, done[0])

                        dve.wait_ge(tot, 1)
                        then(nc.vector.tensor_scalar(mu[:, :], ps_s[0][:, :], 1.0 / N, None, ALU.mult))
                        then(nc.vector.tensor_tensor(var[:, :], mu[:, :], mu[:, :], ALU.mult))
                        dve.wait_ge(tot, 2)
                        then(nc.vector.scalar_tensor_tensor(var[:, :], ps_s[1][:, :], 1.0 / N, var[:, :], ALU.mult, ALU.subtract))
                        nc.vector.tensor_scalar(var[:, :], var[:, :], 0.0, EPS, ALU.max, ALU.add).then_inc(var_ready, 1)
                        dve.wait_ge(dev_ready, 1)
                        then(nc.vector.reciprocal(var[:, :], var[:, :]))
                        dve.wait_ge(tot, 4)
                        then(nc.vector.tensor_tensor(A_bc[:, :], ps_s[2][:, :], var[:, :], ALU.mult))
                        then(nc.vector.tensor_tensor(mu[:, :], mu[:, :], A_bc[:, :], ALU.mult))
                        then(nc.vector.tensor_tensor(C_bc[:, :], ps_s[3][:, :], mu[:, :], ALU.subtract))

                    @block.scalar
                    def _(act):
                        act.wait_ge(var_ready, 1)
                        nc.scalar.activation(var[:, :], var[:, :], ACT.Sqrt).then_inc(dev_ready, 1)

        def attend():
            HA = 5
            with ExitStack() as ctx:
                kv = sb(ctx, "kv", [P, U, G, 2 * D])
                q = sb(ctx, "q", [P, QB * 2 * D], F32R)
                hot = sb(ctx, "hot1", [P, U, G, P], F32R)
                hotT = sb(ctx, "hotT", [P, 2, G * P], F32R)
                score = sb(ctx, "score", [P, U, G * HEADS])
                wgt = sb(ctx, "wgt", [P, U, G * HEADS])
                parts = sb(ctx, "parts", [P, 4, G, 2, HEADS], F32R)
                idx = sb(ctx, "idx1", [P, U // H, H * G], I32)
                ps_q = [pb(ctx, f"ps_q{k}", [P, G * D]) for k in range(2)]
                rel = sb(ctx, "rel1", [P, U // H, H * G])
                ps_h = pb(ctx, "ps_h", [P, 512])
                pss = pb(ctx, "psa", [P, 2 * D])
                psc = pb(ctx, "psw", [P, 512])
                cleared_by, staged, rows_in, q_in = sems("cleared1_", 2), sem("staged1"), sems("rows_in1_", U), sems("q_in", QB)
                hot_made, hot_made_dve, turned, copied, expanded, multiplied = (
                    sem("hot_made1"), sem("hot_made_dve1"), sem("hot_turned"), sem("hot_copied"), sem("expanded"), sem("multiplied"))
                reduced, clipped, weighed, by_act, by_dve = (
                    sem("reduced"), sem("clipped"), sem("weighed"), sem("scaled_by_act"), sem("scaled_by_dve"))
                ps_made, high = sem("ps_made1"), sem("weights_high")

                def steps(i, u, delta):
                    s = i * U + u + delta
                    if isinstance(i, int) and not 0 <= s < STEPS:
                        return None
                    return s, i + (u + delta) // U, (u + delta) % U

                @nc_block()
                def _(block):
                    def times(eng, at, first, last):
                        for t in range(first, 0):
                            at(-1, t + U)
                        for u in range(U):
                            at(0, u)
                        with eng.Fori(1, ITERS - 1) as i:
                            for u in range(U):
                                at(i, u)
                        for u in range(U):
                            at(ITERS - 1, u)
                        for t in range(STEPS, STEPS + last):
                            at(ITERS, t - STEPS)

                    @block.sync
                    def _(sp):
                        def fetch(i, u, regs):
                            s, r = i * U + u, u % QB
                            row, col, new = regs
                            sp.wait_ge(expanded, s + 1)
                            sp.dma_start(q[:, ds(col[u], 2 * D)].bitcast(F32), q_d[ds(row[u], P), :], cond=new[u]).then_inc(q_in[r], 16)

                        with sp.Fori(0, ITERS) as i:
                            regs = [load_values(mybir.EngineType.SP, table, i * U, U, most) for table, most in
                                    ((row_t, (WINDOWS - 1) * P), (qcol_t, (QB - 1) * 2 * D), (new_t, 1))]
                            for u in range(U):
                                fetch(i, u, regs)

                    @block.gpsimd
                    def _(pool):
                        limit = pool.alloc_register("limit1")
                        pool.reg_mov(limit, N - 1)

                        def fetch(i, u):
                            if isinstance(i, int):
                                pool.wait_ge(cleared_by[u % 2], u // 2 + 1)
                            if u % H == 0:
                                pool.wait_ge(staged, i * (U // H) + u // H + 1)
                            pool.wait_ge(ps_made, i * U + u + 1)
                            alone(pool)
                            k = (u % H) * G
                            for g in range(1 + u % 2):
                                last = nc.gpsimd.tensor_scalar(hot[:, u, g, :], lane[:, :], rel[:, u // H, k + g:k + g + 1], None,
                                                               ALU.is_equal)
                            last.then_inc(hot_made, 1)
                            for g in range(G):
                                pool.indirect_dma_start(kv[:, u, g, :], None, kv_d[0:N, :],
                                                        bass.IndirectOffsetOnAxis(idx[:, u // H, k + g:k + g + 1], 0),
                                                        bounds_check=limit, oob_is_err=False).then_inc(rows_in[u], 16)

                        for u in range(U):
                            fetch(0, u)
                        with pool.Fori(1, ITERS) as i:
                            for u in range(U):
                                fetch(i, u)

                    @block.scalar
                    def _(act):
                        act.sem_inc(copied, 1)

                        def stage(i, part):
                            at = ds((i * U + part * H) * G, H * G)
                            nc.scalar.copy(rel[:, part, :], rel_t[:, at])
                            nc.scalar.copy(idx[:, part, :], src_t[:, at]).then_inc(staged, 1)

                        def copy_hot(s, i, u):
                            act.wait_ge(turned, s + 1)
                            act.wait_ge(expanded, s + 3)
                            nc.scalar.copy(hotT[:, u % 2, :], ps_h[:, 0:G * P]).then_inc(copied, 1)

                        def weigh(s, i, u):
                            act.wait_ge(clipped, s + 1)
                            nc.scalar.activation(wgt[:, u, :], score[:, u, :], ACT.Exp).then_inc(weighed, 1)
                            act.wait_ge(weighed, s + 1)
                            act.wait_ge(ps_made, s + U - 3)
                            nc.scalar.copy(parts[:, u % 4, :, 0, :], wgt[:, u, :].rearrange("p (g h) -> p g h", g=G)).then_inc(high, 1)
                            for g in range(G):
                                for h in range(HA):
                                    v = kv[:, u, g, D + h * DH:D + (h + 1) * DH]
                                    last = nc.scalar.mul(v, v, wgt[:, u, g * HEADS + h:g * HEADS + h + 1])
                            last.then_inc(by_act, 1)

                        def restage(i, part):
                            for u in range(part * H, part * H + H):
                                act.wait_ge(rows_in[u], 16 * G * (i + 1))
                            act.wait_ge(hot_made, (i * (U // H) + part + 1) * H)
                            act.wait_ge(hot_made_dve, i * (U // H) + part + 1)
                            alone(act)
                            stage(i + 1, part)

                        def at(i, u):
                            if step := steps(i, u, -1):
                                weigh(*step)
                            if u % H == 0 and u and (not isinstance(i, int) or 0 <= i < ITERS):
                                restage(i, u // H - 1)
                            if u == 0 and (not isinstance(i, int) or 0 < i < ITERS):
                                restage(i - 1, U // H - 1)
                            if step := steps(i, u, 2):
                                copy_hot(*step)

                        for part in range(U // H):
                            stage(0, part)
                        for u in range(1, U, 2):
                            nc.scalar.mul(kv[:, u, :, :].rearrange("p g (a b) -> p (g a) b", b=P),
                                          ones[:, :].unsqueeze(1).to_broadcast([P, G * 2 * D // P, P]), 0.0).then_inc(cleared_by[1], 1)
                        times(act, at, -2, 1)

                    @block.vector
                    def _(dve):
                        for u in range(0, U, 2):
                            nc.vector.memset(kv[:, u, :, :], 0.0).then_inc(cleared_by[0], 1)
                        dve.sem_inc(multiplied, 2)

                        def one_hot(s, i, u):
                            dve.wait_ge(ps_made, s + 1)
                            dve.wait_ge(staged, (s // H if isinstance(s, int) else i * (U // H) + u // H) + 1)
                            nc.vector.tensor_scalar(hot[:, u, 1, :], lane[:, :], rel[:, u // H, (u % H) * G + 1:(u % H) * G + 2],
                                                    None, ALU.is_equal).then_inc(hot_made_dve, 1)

                        def multiply(s, i, u):
                            dve.wait_ge(rows_in[u], 16 * G * (i + 1))
                            dve.wait_ge(expanded, QB + s + 1)
                            k = kv[:, u, :, 0:D]
                            nc.vector.tensor_tensor(k, k, ps_q[u % 2][:, :].rearrange("p (g d) -> p g d", g=G), ALU.mult).then_inc(multiplied, 1)

                        def scale(s, i, u):
                            dve.wait_ge(weighed, s + 1)
                            v = kv[:, u, :, D + HA * DH:2 * D].rearrange("p g (h d) -> p g h d", d=DH)
                            w = wgt[:, u, :].rearrange("p (g h) -> p g h", g=G)[:, :, HA:HEADS]
                            nc.vector.tensor_tensor(v, v, w.unsqueeze(3).to_broadcast([P, G, HEADS - HA, DH]), ALU.mult)
                            dve.wait_ge(high, s + 1)
                            nc.vector.tensor_tensor(parts[:, u % 4, :, 1, :], wgt[:, u, :].rearrange("p (g h) -> p g h", g=G),
                                                    parts[:, u % 4, :, 0, :].bitcast(F32), ALU.subtract).then_inc(by_dve, 1)

                        def reduce(s, i, u):
                            dve.wait_ge(multiplied, s + 3)
                            nc.vector.tensor_reduce(score[:, u, :].rearrange("p (g h) -> p g h", g=G),
                                                    kv[:, u, :, 0:D].rearrange("p g (h d) -> p g h d", h=HEADS),
                                                    AX, ALU.add).then_inc(reduced, 1)

                        def clip(s, i, u):
                            dve.wait_ge(reduced, s + 1)
                            nc.vector.tensor_scalar(score[:, u, :], score[:, u, :], -5.0, 5.0, ALU.max, ALU.min).then_inc(clipped, 1)

                        def flush(s, i, u):
                            if not isinstance(s, int) or s:
                                [new] = load_values(mybir.EngineType.DVE, new_t, s, 1, 1)
                                flush_before(dve, pss, psc, HEADS, s, new, ps_made, U)

                        def at(i, u):
                            if step := steps(i, u, 0):
                                multiply(*step)
                            if step := steps(i, u, -1):
                                scale(*step)
                            if step := steps(i, u, 0):
                                reduce(*step)
                            if (step := steps(i, u, 3)) and step[2] % 2 == 0:
                                one_hot(*step)
                            if step := steps(i, u, -1):
                                flush(*step)
                            if step := steps(i, u, 0):
                                clip(*step)
                            elif not isinstance(i, int) or i == ITERS:
                                nc.vector.memset(score[0:1, 0, 0:1], 0.0).then_inc(clipped, 1)

                        times(dve, at, -3, 1)
                        dve.wait_ge(ps_made, U + STEPS)
                        flush_last(pss, psc, HEADS)

                    @block.tensor
                    def _(pe):
                        pe.sem_inc(ps_made, U)
                        pe.sem_inc(expanded, QB)

                        def turn(s, i, u):
                            pe.wait_ge(hot_made, s + 1)
                            if u % 2 == 0:
                                pe.wait_ge(hot_made_dve, i * (U // 2) + u // 2 + 1)
                            pe.wait_ge(copied, s + 1)
                            for g in range(G):
                                last = nc.tensor.transpose(ps_h[:, g * P:(g + 1) * P], hot[:, u, g, :].bitcast(F32), ident[:, :])
                            last.then_inc(turned, 1)

                        def expand(s, i, u):
                            [col] = load_values(mybir.EngineType.PE, qcol_t, s, 1, (QB - 1) * 2 * D)
                            pe.wait_ge(copied, s + 2)
                            pe.wait_ge(q_in[u % QB], 16 * (i * (U // QB) + u // QB + 1))
                            pe.wait_ge(multiplied, s + 1)
                            for g in range(G):
                                for k in range(2):
                                    last = nc.tensor.matmul(ps_q[u % 2][:, g * D:(g + 1) * D], hotT[:, u % 2, g * P:(g + 1) * P],
                                                            q[:, ds(col + k * D, D)], start=(k == 0), stop=(k == 1))
                            last.then_inc(expanded, 1)

                        def total(s, i, u):
                            [par] = load_values(mybir.EngineType.PE, par_t, s, 1, D)
                            [new] = load_values(mybir.EngineType.PE, new_t, s, 1, 1)
                            pe.wait_ge(clipped, s + 1)
                            open_window(pe, pss, par, new)
                            pe.wait_ge(by_act, s + 1)
                            pe.wait_ge(by_dve, s + 1)
                            for g in range(G):
                                nc.tensor.matmul(pss[:, ds(par, D)], hot[:, u, g, :].bitcast(F32), kv[:, u, g, D:2 * D],
                                                 start=False, stop=(g == G - 1), skip_group_check=True)
                            pe.wait_ge(clipped, s + 2)
                            open_counts(pe, psc, new)
                            for g in range(G):
                                last = nc.tensor.matmul(psc[:, 0:2 * HEADS], hot[:, u, g, :], parts[:, u % 4, g, :, :].rearrange("p t h -> p (t h)"),
                                                        start=False, stop=(g == G - 1), skip_group_check=True)
                            last.then_inc(ps_made, 1)

                        def at(i, u):
                            if step := steps(i, u, -2):
                                total(*step)
                            if step := steps(i, u, 2):
                                turn(*step)
                            if step := steps(i, u, 1):
                                expand(*step)

                        times(pe, at, -2, 2)

        def attended(S1, S2):
            with ExitStack() as ctx:
                h1 = sb(ctx, "h1b", [P, NB, D])
                sq = sb(ctx, "sq1", [P, NB, D])
                ps_1 = pb(ctx, "ps_1", [P, 512])
                zero2, h_in, inverse, weighted, made, squared, summed1, summed2 = (
                    sem("zeroed_S2"), sems("h_in2", NB), sem("inverse"), sem("weighted"), sem("h_made2"), sem("squared1"),
                    sem("summed1b"), sem("summed2b"))

                @nc_block()
                def _(block):
                    @block.sync
                    def _(sp):
                        def load(w, b):
                            sp.wait_ge(made, w + 1)
                            sp.dma_start(h1[:, b, :], h1_d[ds(w * P, P), :]).then_inc(h_in[b], 16)

                        with sp.Fori(0, FOURS) as i:
                            for b in range(NB):
                                load(NB * i + b, b)
                        load(WINDOWS - 1, 0)

                    @block.gpsimd
                    def _(pool):
                        nc.gpsimd.memset(S2[:, :], 0.0).then_inc(zero2, 1)
                        pool.wait_ge(zero2, 1)

                        def add_square(w, b, n=P):
                            pool.wait_ge(squared, w + 1)
                            nc.gpsimd.tensor_tensor(S2[0:n, :], S2[0:n, :], sq[0:n, b, :], ALU.add).then_inc(summed2, 1)
                            pool.wait_ge(summed2, w + 1)

                        with pool.Fori(0, FOURS) as i:
                            for b in range(NB):
                                add_square(NB * i + b, b)
                        add_square(WINDOWS - 1, 0, LAST)

                    @block.tensor
                    def _(pe):
                        column_sums(pe, ps_1, made, NB, summed1)

                    @block.scalar
                    def _(act):
                        def square(w, b):
                            act.wait_ge(made, w + NB + 1)
                            if not isinstance(w, int) or w >= NB:
                                act.wait_ge(summed2, w - NB + 1)
                            alone(act)
                            nc.scalar.activation(sq[:, b, :], window(w), ACT.Square).then_inc(squared, 1)

                        for w in range(NB):
                            square(w, w)
                        with act.Fori(1, FOURS) as i:
                            for b in range(NB):
                                square(NB * i + b, b)
                        square(WINDOWS - 1, 0)

                    @block.vector
                    def _(dve):
                        dve.sem_inc(made, NB)
                        weights = sums[:, :].rearrange("p (w c) -> p w c", c=WIDTH)[:, :, D:WIDTH]
                        nc.vector.tensor_scalar(weights, weights, 1e-6, None, ALU.add).then_inc(inverse, 1)
                        dve.wait_ge(inverse, 1)
                        nc.vector.reciprocal(weights, weights).then_inc(inverse, 1)
                        dve.wait_ge(inverse, 2)

                        def weight(w):
                            v = window(w).rearrange("p (h d) -> p h d", h=HEADS)
                            z = sums[:, ds(w * WIDTH + D, HEADS)].unsqueeze(2).to_broadcast([P, HEADS, DH])
                            nc.vector.tensor_tensor(v, v, z, ALU.mult).then_inc(weighted, 1)

                        def add_h1(w, i, b):
                            dve.wait_ge(h_in[b], 16 * (i + 1))
                            dve.wait_ge(weighted, w + 1)
                            nc.vector.tensor_tensor(window(w), window(w), h1[:, b, :], ALU.add).then_inc(made, 1)

                        weight(0)
                        with dve.Fori(0, FOURS) as i:
                            for b in range(NB):
                                weight(NB * i + b + 1)
                                add_h1(NB * i + b, i, b)
                        add_h1(WINDOWS - 1, FOURS, 0)
                        dve.wait_ge(summed1, WINDOWS)
                        share_of(S1, ps_1)

        def finish(A_bc, C_bc):
            with ExitStack() as ctx:
                x1 = sb(ctx, "x1b", [P, NB, D])
                o = sb(ctx, "o", [P, NB, D])
                x_in, shifted, scaled, done, stored = sems("x_in3", NB), sem("shifted"), sem("scaled1"), sem("done"), sems("stored_", NB)

                @nc_block()
                def _(block):
                    @block.sync
                    def _(sp):
                        def load(w, b):
                            sp.wait_ge(done, w + 1)
                            sp.dma_start(x1[:, b, :], x1_d[ds(w * P, P), :]).then_inc(x_in[b], 16)

                        with sp.Fori(0, FOURS) as i:
                            for b in range(NB):
                                load(NB * i + b, b)
                        load(WINDOWS - 1, 0)

                    @block.scalar
                    def _(act):
                        def store(w, b, n=P):
                            act.wait_ge(done, w + NB + 1)
                            act.dma_start(out[ds(w * P, n), :], o[0:n, b, :]).then_inc(stored[b], 16)

                        with act.Fori(0, FOURS) as i:
                            for b in range(NB):
                                store(NB * i + b, b)
                        store(WINDOWS - 1, 0, LAST)
                        for b in range(NB):
                            act.wait_ge(stored[b], 16 * (FOURS + (b == 0)))

                    @block.gpsimd
                    def _(pool):
                        def shift(w, i, b):
                            pool.wait_ge(x_in[b], 16 * (i + 1))
                            nc.gpsimd.tensor_tensor(x1[:, b, :], x1[:, b, :], C_bc[:, :], ALU.add).then_inc(shifted, 1)

                        with pool.Fori(0, FOURS) as i:
                            for b in range(NB):
                                shift(NB * i + b, i, b)
                        shift(WINDOWS - 1, FOURS, 0)

                    @block.vector
                    def _(dve):
                        dve.sem_inc(done, NB)

                        def scale(w):
                            nc.vector.tensor_tensor(window(w), window(w), A_bc[:, :], ALU.mult).then_inc(scaled, 1)

                        def add(w, i, b):
                            dve.wait_ge(shifted, w + 1)
                            dve.wait_ge(scaled, w + 1)
                            if not isinstance(i, int) or i:
                                dve.wait_ge(stored[b], 16 * i)
                            nc.vector.tensor_tensor(o[:, b, :], window(w), x1[:, b, :], ALU.add).then_inc(done, 1)

                        scale(0)
                        for w in range(NB):
                            scale(w + 1)
                            add(w, 0, w)
                        with dve.Fori(1, FOURS) as i:
                            for b in range(NB):
                                scale(NB * i + b + 1)
                                add(NB * i + b, i, b)
                        add(WINDOWS - 1, FOURS, 0)

        prepare()
        dense(0, (W_l, W_r))
        aggregate()
        batch_norm("0", combine, gamma0, beta0, lambda A, C: dense(1, (Wq, Wk, Wv), A, C))
        attend()
        batch_norm("1", attended, gamma1, beta1, finish)


def kernel(**inputs):
    import numpy as np
    import concourse.bacc as bacc
    from concourse.bass_utils import run_bass_kernel_spmd

    names = ["x", "src", "dst", "L0_gnn_W_l", "L0_gnn_b_l", "L0_gnn_W_r", "L0_gnn_gamma", "L0_gnn_beta",
             "L1_gnn_Wq", "L1_gnn_Wk", "L1_gnn_Wv", "L1_gnn_bn_gamma", "L1_gnn_bn_beta"]
    nc = bacc.Bacc("TRN2", target_bir_lowering=False, num_devices=1)
    arrays, args = {}, []
    for name in names:
        a = np.ascontiguousarray(inputs[name])
        arrays["in_" + name] = a
        args.append(nc.dram_tensor("in_" + name, a.shape, mybir.dt.from_np(a.dtype), kind="ExternalInput").ap())
    shape = inputs["x"].shape
    result = nc.dram_tensor("result", shape, F32, kind="ExternalOutput").ap()
    build(nc, *args, result)
    r = run_bass_kernel_spmd(nc, [arrays], core_ids=[0])
    return r.results[0]["result"]
```
